# Optimizing a Trainium2 kernel written in Bass

```python
import numpy as np
import jax
import jax.numpy as jnp

def _softmax(x, axis=-1):
    return jax.nn.softmax(x, axis=axis)

def _gelu(x):
    return jax.nn.gelu(x, approximate=True)

def _silu(x):
    return jax.nn.silu(x)

def _sigmoid(x):
    return jax.nn.sigmoid(x)

def _layernorm(x, axis=-1, eps=1e-05):
    m = jnp.mean(x, axis=axis, keepdims=True)
    v = jnp.var(x, axis=axis, keepdims=True)
    return (x - m) / jnp.sqrt(v + eps)

def _scatter_add(tgt, idx, src, axis=0):
    return tgt.at[idx].add(src)

def _segment_sum(src, seg, n):
    return jax.ops.segment_sum(src, seg, n)
kernel_name = 'mk_seq_preln_d1_jaxref_r8_37db40'

def setup_inputs(seed: int=0):
    np.random.seed(seed)
    _w = jnp.asarray

    def _L0_attn_setup():
        import jax, jax.numpy as jnp
        import numpy as np
        B, T, C, H = (8, 64, 128, 16)
        N = C // H
        DW, DA, DG = (64, 64, 128)

        def _ln(x, w, b, eps=1e-05):
            mu = x.mean(-1, keepdims=True)
            var = ((x - mu) ** 2).mean(-1, keepdims=True)
            return (x - mu) * jax.lax.rsqrt(var + eps) * w + b

        def _gn_heads(x, w, b, eps=0.00064):
            xh = x.reshape(x.shape[0], x.shape[1], H, N)
            mu = xh.mean(-1, keepdims=True)
            var = ((xh - mu) ** 2).mean(-1, keepdims=True)
            xh = (xh - mu) * jax.lax.rsqrt(var + eps)
            return xh.reshape(x.shape) * w + b

        def _shift(x):
            return jnp.concatenate([jnp.zeros_like(x[:, :1]), x[:, :-1]], axis=1)

        def _wkv7(r, w_log, k, v, a, b):
            decay = jnp.exp(-jnp.exp(w_log))

            def step(state, inp):
                r_t, d_t, k_t, v_t, a_t, b_t = inp
                sa = jnp.einsum('bhij,bhj->bhi', state, a_t)
                state = state * d_t[:, :, None, :] + sa[..., None] * b_t[:, :, None, :] + v_t[..., None] * k_t[:, :, None, :]
                return (state, jnp.einsum('bhij,bhj->bhi', state, r_t))
            xs = tuple((jnp.moveaxis(t, 1, 0) for t in (r, decay, k, v, a, b)))
            s0 = jnp.zeros((r.shape[0], H, N, N), r.dtype)
            _, out = jax.lax.scan(step, s0, xs)
            return jnp.moveaxis(out, 0, 1)

        def _reference_tuple_inner(x, v_first, ln_pre_w, ln_pre_b, ln_attn_w, ln_attn_b, ln_ffn_w, ln_ffn_b, x_r, x_w, x_k, x_v, x_a, x_g, w0, w1, w2, a0, a1, a2, g1, g2, k_k, k_a, r_k, W_r, W_k, W_v, W_o, gn_w, gn_b, ffn_x_k, W_ffn1, W_ffn2):
            Bx, Tx = (x.shape[0], x.shape[1])
            x = _ln(x, ln_pre_w, ln_pre_b)
            xn = _ln(x, ln_attn_w, ln_attn_b)
            dx = _shift(xn) - xn
            xr = xn + dx * x_r
            xw = xn + dx * x_w
            xk = xn + dx * x_k
            xv = xn + dx * x_v
            xa = xn + dx * x_a
            xg = xn + dx * x_g
            r = xr @ W_r
            w_log = -jax.nn.softplus(-(w0 + jnp.tanh(xw @ w1) @ w2)) - 0.5
            k = xk @ W_k
            v = xv @ W_v
            v_first = v
            a = jax.nn.sigmoid(a0 + xa @ a1 @ a2)
            g = jax.nn.sigmoid(xg @ g1) @ g2
            kk = (k * k_k).reshape(Bx, Tx, H, N)
            kk = kk / jnp.maximum(jnp.linalg.norm(kk, axis=-1, keepdims=True), 1e-12)
            k = k * (1.0 + (a - 1.0) * k_a)
            rh = r.reshape(Bx, Tx, H, N)
            kh = k.reshape(Bx, Tx, H, N)
            vh = v.reshape(Bx, Tx, H, N)
            ah = a.reshape(Bx, Tx, H, N)
            o = _wkv7(rh, w_log.reshape(Bx, Tx, H, N), kh, vh, -kk, kk * ah)
            o = _gn_heads(o.reshape(Bx, Tx, C), gn_w, gn_b)
            o = o + ((rh * kh * r_k).sum(-1, keepdims=True) * vh).reshape(Bx, Tx, C)
            x = x + o * g @ W_o
            xf = _ln(x, ln_ffn_w, ln_ffn_b)
            kf = xf + (_shift(xf) - xf) * ffn_x_k
            x = x + jnp.square(jax.nn.relu(kf @ W_ffn1)) @ W_ffn2
            return (x, v_first)
        key = jax.random.key(seed)
        ks = iter(jax.random.split(key, 40))

        def nrm(shape, s=0.02):
            return jax.random.normal(next(ks), shape, jnp.float32) * s
        f32 = jnp.float32
        d = {'x': jax.random.normal(next(ks), (B, T, C), f32), 'v_first': jnp.zeros((B, T, C), f32), 'ln_pre_w': jnp.ones((C,), f32), 'ln_pre_b': jnp.zeros((C,), f32), 'ln_attn_w': jnp.ones((C,), f32), 'ln_attn_b': jnp.zeros((C,), f32), 'ln_ffn_w': jnp.ones((C,), f32), 'ln_ffn_b': jnp.zeros((C,), f32), 'x_r': nrm((C,), 0.1), 'x_w': nrm((C,), 0.1), 'x_k': nrm((C,), 0.1), 'x_v': nrm((C,), 0.1), 'x_a': nrm((C,), 0.1), 'x_g': nrm((C,), 0.1), 'w0': nrm((C,), 0.5), 'w1': nrm((C, DW)), 'w2': nrm((DW, C)), 'a0': nrm((C,), 0.1), 'a1': nrm((C, DA)), 'a2': nrm((DA, C)), 'g1': nrm((C, DG)), 'g2': nrm((DG, C)), 'k_k': 0.85 * jnp.ones((C,), f32) + nrm((C,), 0.05), 'k_a': jnp.ones((C,), f32), 'r_k': nrm((H, N), 0.1), 'W_r': nrm((C, C)), 'W_k': nrm((C, C)), 'W_v': nrm((C, C)), 'W_o': nrm((C, C)), 'gn_w': jnp.ones((C,), f32), 'gn_b': jnp.zeros((C,), f32), 'ffn_x_k': nrm((C,), 0.1), 'W_ffn1': nrm((C, 4 * C)), 'W_ffn2': nrm((4 * C, C))}
        return d
    _L0_attn_in = _L0_attn_setup()

    def _L0_ffn_setup():
        import jax, jax.numpy as jnp
        import numpy as np
        H = 128
        I = 512
        E = 4
        LN_EPS = 1e-12

        def _layer_norm(x, gamma, beta, eps=LN_EPS):
            mu = jnp.mean(x, axis=-1, keepdims=True)
            var = jnp.mean(jnp.square(x - mu), axis=-1, keepdims=True)
            return (x - mu) * jax.lax.rsqrt(var + eps) * gamma + beta
        key = jax.random.key(seed)
        ks = jax.random.split(key, 8)
        B, S = (4, 64)
        scale = 0.02
        return {'hidden_states': jax.random.normal(ks[0], (B, S, H), jnp.float32), 'W_router': jax.random.normal(ks[1], (H, E), jnp.float32) * scale, 'W1': jax.random.normal(ks[2], (E, H, I), jnp.float32) * scale, 'b1': jax.random.normal(ks[3], (E, I), jnp.float32) * scale, 'Wo': jax.random.normal(ks[4], (I, H), jnp.float32) * scale, 'bo': jax.random.normal(ks[5], (H,), jnp.float32) * scale, 'ln_gamma': jnp.ones((H,), jnp.float32), 'ln_beta': jnp.zeros((H,), jnp.float32)}
    _L0_ffn_in = _L0_ffn_setup()
    _d = {'L0_attn_x': _L0_attn_in['x'], 'L0_attn_v_first': _L0_attn_in['v_first'], 'L0_attn_ln_pre_w': _L0_attn_in['ln_pre_w'], 'L0_attn_ln_pre_b': _L0_attn_in['ln_pre_b'], 'L0_attn_ln_attn_w': _L0_attn_in['ln_attn_w'], 'L0_attn_ln_attn_b': _L0_attn_in['ln_attn_b'], 'L0_attn_ln_ffn_w': _L0_attn_in['ln_ffn_w'], 'L0_attn_ln_ffn_b': _L0_attn_in['ln_ffn_b'], 'L0_attn_x_r': _L0_attn_in['x_r'], 'L0_attn_x_w': _L0_attn_in['x_w'], 'L0_attn_x_k': _L0_attn_in['x_k'], 'L0_attn_x_v': _L0_attn_in['x_v'], 'L0_attn_x_a': _L0_attn_in['x_a'], 'L0_attn_x_g': _L0_attn_in['x_g'], 'L0_attn_w0': _L0_attn_in['w0'], 'L0_attn_w1': _L0_attn_in['w1'], 'L0_attn_w2': _L0_attn_in['w2'], 'L0_attn_a0': _L0_attn_in['a0'], 'L0_attn_a1': _L0_attn_in['a1'], 'L0_attn_a2': _L0_attn_in['a2'], 'L0_attn_g1': _L0_attn_in['g1'], 'L0_attn_g2': _L0_attn_in['g2'], 'L0_attn_k_k': _L0_attn_in['k_k'], 'L0_attn_k_a': _L0_attn_in['k_a'], 'L0_attn_r_k': _L0_attn_in['r_k'], 'L0_attn_W_r': _L0_attn_in['W_r'], 'L0_attn_W_k': _L0_attn_in['W_k'], 'L0_attn_W_v': _L0_attn_in['W_v'], 'L0_attn_W_o': _L0_attn_in['W_o'], 'L0_attn_gn_w': _L0_attn_in['gn_w'], 'L0_attn_gn_b': _L0_attn_in['gn_b'], 'L0_attn_ffn_x_k': _L0_attn_in['ffn_x_k'], 'L0_attn_W_ffn1': _L0_attn_in['W_ffn1'], 'L0_attn_W_ffn2': _L0_attn_in['W_ffn2'], 'L0_ffn_W_router': _L0_ffn_in['W_router'], 'L0_ffn_W1': _L0_ffn_in['W1'], 'L0_ffn_b1': _L0_ffn_in['b1'], 'L0_ffn_Wo': _L0_ffn_in['Wo'], 'L0_ffn_bo': _L0_ffn_in['bo'], 'L0_ffn_ln_gamma': _L0_ffn_in['ln_gamma'], 'L0_ffn_ln_beta': _L0_ffn_in['ln_beta']}
    _x0 = _d['L0_attn_x']
    _d['L0_attn_x'] = jax.random.normal(jax.random.fold_in(jax.random.key(seed), 1), (16, 512, 128), dtype=_x0.dtype)
    del _x0
    return _d

def reference(L0_attn_x, L0_attn_v_first, L0_attn_ln_pre_w, L0_attn_ln_pre_b, L0_attn_ln_attn_w, L0_attn_ln_attn_b, L0_attn_ln_ffn_w, L0_attn_ln_ffn_b, L0_attn_x_r, L0_attn_x_w, L0_attn_x_k, L0_attn_x_v, L0_attn_x_a, L0_attn_x_g, L0_attn_w0, L0_attn_w1, L0_attn_w2, L0_attn_a0, L0_attn_a1, L0_attn_a2, L0_attn_g1, L0_attn_g2, L0_attn_k_k, L0_attn_k_a, L0_attn_r_k, L0_attn_W_r, L0_attn_W_k, L0_attn_W_v, L0_attn_W_o, L0_attn_gn_w, L0_attn_gn_b, L0_attn_ffn_x_k, L0_attn_W_ffn1, L0_attn_W_ffn2, L0_ffn_W_router, L0_ffn_W1, L0_ffn_b1, L0_ffn_Wo, L0_ffn_bo, L0_ffn_ln_gamma, L0_ffn_ln_beta):

    def _L0_attn_ref(x, v_first, ln_pre_w, ln_pre_b, ln_attn_w, ln_attn_b, ln_ffn_w, ln_ffn_b, x_r, x_w, x_k, x_v, x_a, x_g, w0, w1, w2, a0, a1, a2, g1, g2, k_k, k_a, r_k, W_r, W_k, W_v, W_o, gn_w, gn_b, ffn_x_k, W_ffn1, W_ffn2):
        import jax, jax.numpy as jnp
        import numpy as np
        B, T, C, H = (8, 64, 128, 16)
        N = C // H
        DW, DA, DG = (64, 64, 128)

        def _ln(x, w, b, eps=1e-05):
            mu = x.mean(-1, keepdims=True)
            var = ((x - mu) ** 2).mean(-1, keepdims=True)
            return (x - mu) * jax.lax.rsqrt(var + eps) * w + b

        def _gn_heads(x, w, b, eps=0.00064):
            xh = x.reshape(x.shape[0], x.shape[1], H, N)
            mu = xh.mean(-1, keepdims=True)
            var = ((xh - mu) ** 2).mean(-1, keepdims=True)
            xh = (xh - mu) * jax.lax.rsqrt(var + eps)
            return xh.reshape(x.shape) * w + b

        def _shift(x):
            return jnp.concatenate([jnp.zeros_like(x[:, :1]), x[:, :-1]], axis=1)

        def _wkv7(r, w_log, k, v, a, b):
            decay = jnp.exp(-jnp.exp(w_log))

            def step(state, inp):
                r_t, d_t, k_t, v_t, a_t, b_t = inp
                sa = jnp.einsum('bhij,bhj->bhi', state, a_t)
                state = state * d_t[:, :, None, :] + sa[..., None] * b_t[:, :, None, :] + v_t[..., None] * k_t[:, :, None, :]
                return (state, jnp.einsum('bhij,bhj->bhi', state, r_t))
            xs = tuple((jnp.moveaxis(t, 1, 0) for t in (r, decay, k, v, a, b)))
            s0 = jnp.zeros((r.shape[0], H, N, N), r.dtype)
            _, out = jax.lax.scan(step, s0, xs)
            return jnp.moveaxis(out, 0, 1)

        def _reference_tuple_inner(x, v_first, ln_pre_w, ln_pre_b, ln_attn_w, ln_attn_b, ln_ffn_w, ln_ffn_b, x_r, x_w, x_k, x_v, x_a, x_g, w0, w1, w2, a0, a1, a2, g1, g2, k_k, k_a, r_k, W_r, W_k, W_v, W_o, gn_w, gn_b, ffn_x_k, W_ffn1, W_ffn2):
            Bx, Tx = (x.shape[0], x.shape[1])
            x = _ln(x, ln_pre_w, ln_pre_b)
            xn = _ln(x, ln_attn_w, ln_attn_b)
            dx = _shift(xn) - xn
            xr = xn + dx * x_r
            xw = xn + dx * x_w
            xk = xn + dx * x_k
            xv = xn + dx * x_v
            xa = xn + dx * x_a
            xg = xn + dx * x_g
            r = xr @ W_r
            w_log = -jax.nn.softplus(-(w0 + jnp.tanh(xw @ w1) @ w2)) - 0.5
            k = xk @ W_k
            v = xv @ W_v
            v_first = v
            a = jax.nn.sigmoid(a0 + xa @ a1 @ a2)
            g = jax.nn.sigmoid(xg @ g1) @ g2
            kk = (k * k_k).reshape(Bx, Tx, H, N)
            kk = kk / jnp.maximum(jnp.linalg.norm(kk, axis=-1, keepdims=True), 1e-12)
            k = k * (1.0 + (a - 1.0) * k_a)
            rh = r.reshape(Bx, Tx, H, N)
            kh = k.reshape(Bx, Tx, H, N)
            vh = v.reshape(Bx, Tx, H, N)
            ah = a.reshape(Bx, Tx, H, N)
            o = _wkv7(rh, w_log.reshape(Bx, Tx, H, N), kh, vh, -kk, kk * ah)
            o = _gn_heads(o.reshape(Bx, Tx, C), gn_w, gn_b)
            o = o + ((rh * kh * r_k).sum(-1, keepdims=True) * vh).reshape(Bx, Tx, C)
            x = x + o * g @ W_o
            xf = _ln(x, ln_ffn_w, ln_ffn_b)
            kf = xf + (_shift(xf) - xf) * ffn_x_k
            x = x + jnp.square(jax.nn.relu(kf @ W_ffn1)) @ W_ffn2
            return (x, v_first)
        return _reference_tuple_inner(x, v_first, ln_pre_w, ln_pre_b, ln_attn_w, ln_attn_b, ln_ffn_w, ln_ffn_b, x_r, x_w, x_k, x_v, x_a, x_g, w0, w1, w2, a0, a1, a2, g1, g2, k_k, k_a, r_k, W_r, W_k, W_v, W_o, gn_w, gn_b, ffn_x_k, W_ffn1, W_ffn2)[0]

    def _L0_ffn_ref(hidden_states, W_router, W1, b1, Wo, bo, ln_gamma, ln_beta):
        import jax, jax.numpy as jnp
        import numpy as np
        H = 128
        I = 512
        E = 4
        LN_EPS = 1e-12

        def _layer_norm(x, gamma, beta, eps=LN_EPS):
            mu = jnp.mean(x, axis=-1, keepdims=True)
            var = jnp.mean(jnp.square(x - mu), axis=-1, keepdims=True)
            return (x - mu) * jax.lax.rsqrt(var + eps) * gamma + beta
        B, S, _ = hidden_states.shape
        x = hidden_states.reshape(-1, H)
        logits = x @ W_router
        expert_idx = jnp.argmax(logits, axis=-1)
        h = jnp.einsum('th,ehi->tei', x, W1) + b1
        h = jax.nn.gelu(h, approximate=False)
        onehot = jax.nn.one_hot(expert_idx, E, dtype=x.dtype)
        intermediate = jnp.einsum('te,tei->ti', onehot, h)
        y = intermediate @ Wo + bo + x
        y = _layer_norm(y, ln_gamma, ln_beta)
        return y.reshape(B, S, H)
    x = L0_attn_x
    x = x + _L0_attn_ref(_layernorm(x, axis=-1), L0_attn_v_first, L0_attn_ln_pre_w, L0_attn_ln_pre_b, L0_attn_ln_attn_w, L0_attn_ln_attn_b, L0_attn_ln_ffn_w, L0_attn_ln_ffn_b, L0_attn_x_r, L0_attn_x_w, L0_attn_x_k, L0_attn_x_v, L0_attn_x_a, L0_attn_x_g, L0_attn_w0, L0_attn_w1, L0_attn_w2, L0_attn_a0, L0_attn_a1, L0_attn_a2, L0_attn_g1, L0_attn_g2, L0_attn_k_k, L0_attn_k_a, L0_attn_r_k, L0_attn_W_r, L0_attn_W_k, L0_attn_W_v, L0_attn_W_o, L0_attn_gn_w, L0_attn_gn_b, L0_attn_ffn_x_k, L0_attn_W_ffn1, L0_attn_W_ffn2)
    x = x + _L0_ffn_ref(_layernorm(x, axis=-1), L0_ffn_W_router, L0_ffn_W1, L0_ffn_b1, L0_ffn_Wo, L0_ffn_bo, L0_ffn_ln_gamma, L0_ffn_ln_beta)
    return x

_drawn_inputs = setup_inputs


def setup_inputs(seed=0):
    import zlib

    import numpy as np

    out = dict(_drawn_inputs(seed))
    spreads = {'L0_attn_v_first': (0.0, 0.1),
     'L0_attn_ln_pre_w': (1.0, 0.2),
     'L0_attn_ln_pre_b': (0.0, 0.1),
     'L0_attn_ln_attn_w': (1.0, 0.6),
     'L0_attn_ln_attn_b': (0.0, 0.8),
     'L0_attn_ln_ffn_w': (1.0, 0.6),
     'L0_attn_ln_ffn_b': (0.0, 2.0),
     'L0_attn_k_a': (1.0, 0.6),
     'L0_attn_gn_w': (1.0, 0.6),
     'L0_attn_gn_b': (0.0, 2.0),
     'L0_ffn_ln_gamma': (1.0, 0.6),
     'L0_ffn_ln_beta': (0.0, 0.8)}
    factors = {'L0_attn_x_r': 8.0,
     'L0_attn_x_w': 64.0,
     'L0_attn_x_k': 8.0,
     'L0_attn_x_v': 8.0,
     'L0_attn_x_a': 8.0,
     'L0_attn_x_g': 8.0,
     'L0_attn_w0': 64.0,
     'L0_attn_w1': 64.0,
     'L0_attn_w2': 64.0,
     'L0_attn_a0': 8.0,
     'L0_attn_a1': 8.0,
     'L0_attn_a2': 8.0,
     'L0_attn_g1': 8.0,
     'L0_attn_g2': 7.425,
     'L0_attn_k_k': 64.0,
     'L0_attn_r_k': 8.0,
     'L0_attn_W_r': 7.389,
     'L0_attn_W_k': 7.401,
     'L0_attn_W_v': 7.432,
     'L0_attn_W_o': 7.332,
     'L0_attn_ffn_x_k': 8.0,
     'L0_attn_W_ffn1': 3.961,
     'L0_attn_W_ffn2': 3.625,
     'L0_ffn_W_router': 29.176,
     'L0_ffn_W1': 25.336,
     'L0_ffn_b1': 64.0,
     'L0_ffn_Wo': 24.816,
     'L0_ffn_bo': 55.784}
    for name, (base, spread) in spreads.items():
        noise = np.random.default_rng([zlib.crc32(name.encode()), seed]).standard_normal(out[name].shape)
        drawn = base * np.exp(spread * noise) if base else spread * noise
        out[name] = jnp.asarray(drawn.astype(out[name].dtype))
    for name, factor in factors.items():
        out[name] = (out[name] * factor).astype(out[name].dtype)
    return out
```

```python
from contextlib import ExitStack

import numpy as np
import concourse.bass as bass
from concourse import mybir

F32 = mybir.dt.float32
BF16 = mybir.dt.bfloat16
ALU = mybir.AluOpType
ACT = mybir.ActivationFunctionType
AX = mybir.AxisListType

B, T, C = 16, 512, 128
H, N = 16, 8
STEPS = 32
COLS = STEPS * B
CHUNKS = T // STEPS
QUARTER = 8
QCOLS = QUARTER * B
QUARTERS = STEPS // QUARTER
STATE = N * B
E, I = 4, 512
J = I // C
RING = 3
DW = 64
DECAY = float(np.exp(-0.5))

VECS = ["ln_pre_w", "ln_pre_b", "ln_attn_w", "ln_attn_b", "ln_ffn_w", "ln_ffn_b",
        "x_r", "x_w", "x_k", "x_v", "x_a", "x_g", "w0", "a0", "k_k", "k_a", "r_k",
        "gn_w", "gn_b", "ffn_x_k"]
FFN_VECS = ["bo", "ln_gamma", "ln_beta"]
V = {name: n for n, name in enumerate(VECS + FFN_VECS)}
NV = len(V)

M = {}
_at = 0
for _name, _w in [("W_k", C), ("w1", DW), ("a1", DW), ("W_v", C), ("W_r", C), ("g1", C), ("g2", C), ("W_o", C), ("w2_a2", C),
                  ("ffn1", J * C), ("ffn2", J * C), ("router", E), ("W1", E * I), ("Wo", J * C)]:
    M[_name] = _at
    _at += _w
NM = _at

K = {}
_at = 0
for _name, _w in [("center", C), ("mean", C), ("center8", C), ("mean8", C), ("sum8", C), ("ident", C),
                  ("spread", N * C), ("gather", N * C), ("rank", 4 * E)]:
    K[_name] = _at
    _at += _w
NK = _at


class Chunk:

    def __init__(self, base, off):
        self.base, self.off = base, off
        self.slot = off % RING

    def __add__(self, n):
        return Chunk(self.base, self.off + n)

    def has(self, back=0):
        return not isinstance(self.base, int) or 0 <= self.off - back < CHUNKS

    def count(self, done=1, per=1):
        if isinstance(self.base, int):
            return self.off * per + done
        return self.base * per + (self.off * per + done)

    def cols(self, eng):
        if isinstance(self.base, int):
            return slice(self.off * COLS, (self.off + 1) * COLS)
        return bass.ds(eng.snap(self.base * COLS + self.off * COLS), COLS)


def settled(eng, value):
    return value if isinstance(value, int) else eng.to_reg(value)


class Part:

    def __init__(self, pieces):
        self.pieces, self.at = pieces, -1

    def upto(self, step):
        while self.at <= step:
            self.at = next(self.pieces, 10 ** 6)


def build(nc, xT, mats, vecs, consts, b1_in, out):
    with ExitStack() as ctx:
        def sb(name, cols, dtype=F32, rows=128):
            return ctx.enter_context(nc.sbuf_tensor(name, [rows, cols], dtype))

        def ring(name, cols):
            return [sb(f"{name}{n}", cols) for n in range(RING)]

        def single(name, cols):
            return [sb(name, cols)] * RING

        def bank(name):
            return ctx.enter_context(nc.psum_tensor(name, [128, 512], F32))

        def sem(name):
            return ctx.enter_context(nc.semaphore(name))

        mat, vec, con = sb("mat", NM), sb("vec", NV), sb("con", NK)
        half_w0, half_a0, half_ka, rest_ka = (sb(n, 1) for n in ("half_w0", "half_a0", "half_ka", "rest_ka"))
        ident_bf = sb("ident_bf", C, BF16)
        b1_rows, b1_rest = sb("b1_rows", I, rows=E), sb("b1_rest", I, rows=E)
        b1_parts = [sb(f"b1_part{n}", I, BF16, rows=E) for n in range(3)]
        scan_keep = sb("scan_keep", COLS)
        eps = {1e-5: sb("eps_ln", 1), 1e-5 ** 2: sb("eps_sq", 1), 6.4e-4: sb("eps_gn", 1), 1e-12: sb("eps_last", 1)}
        eps_ln, eps_sq, eps_gn, eps_last = (tile[:] for tile in eps.values())

        def w(name, n=0, width=C):
            return mat[:, M[name] + n * width:M[name] + (n + 1) * width]

        def k(name, n=0, width=C):
            return con[:, K[name] + n * width:K[name] + (n + 1) * width]

        def v(name):
            return vec[:, V[name]:V[name] + 1]

        x_in, x_res = single("x_in", COLS), single("x_res", COLS)
        x1, xn = ring("x1", COLS), single("xn", B + COLS)
        a_t, b_t, k_t, r_t = ring("a_t", COLS), ring("b_t", COLS), ring("k_t", COLS), ring("r_t", COLS)
        p_all = ring("p_all", B + COLS)
        val, gate, bonus = ring("val", COLS), ring("gate", COLS), ring("bonus", COLS)
        xf, x2x = single("xf", B + COLS), single("x2x", COLS)

        sq_p, lv_p, rs_p, xh_p = (sb(n, COLS) for n in ("sq_p", "lv_p", "rs_p", "xh_p"))
        dx = sb("dx", COLS)
        mix = {q: sb(f"mix_{q}", COLS) for q in "wkag"}
        mix["v"], mix["r"] = mix["w"], mix["k"]
        key, k2, th_g, dec_bt, cum_bt = (sb(n, COLS) for n in ("key", "k2", "th_g", "dec_bt", "cum_bt"))
        low = sb("low", COLS)
        th_w, low_a = low[0:DW, :], low[DW:2 * DW, :]
        rkb, kk, kki, inv_p, th_a, rec = mix["w"], mix["a"], mix["g"], dec_bt, dx, xh_p
        state = sb("state", (STEPS + 1) * STATE)
        s_a, upd, plus_kv = sb("s_a", STATE), sb("upd", STATE), sb("plus_kv", 2 * STATE)
        kv = sb("kv", 2 * QUARTER * STATE)
        s_r = sb("s_r", 2 * QUARTER * STATE)
        o_sb, sq_m, rs_m, y_m, z_m = (sb(n, COLS) for n in ("o_sb", "sq_m", "rs_m", "y_m", "z_m"))
        x2, kf = o_sb, z_m
        hid = [sb(f"hid{j}", COLS) for j in range(J)]
        y1, y1b, h, sq_f, rs_f = (sb(n, COLS) for n in ("y1", "y1b", "h", "sq_f", "rs_f"))
        best, score, best2 = sb("best", 4), sb("score", 4 * E), sb("best2", 4)
        eq = sb("eq", 4 * E)
        onehot = sb("onehot", 4 * E, BF16)
        pick = sb("pick", COLS, BF16, rows=E)
        h_e = [sb(f"h_e{e}", COLS) for e in range(E)]
        act_j, y2 = hid, h_e[0]
        res = single("res", COLS)

        sa_ps, o_ps, vb_ps = bank("sa_ps"), bank("o_ps"), bank("vb_ps")
        pre_a, pre_b, mid_ps, fin_a, fin_b = (bank(n) for n in ("pre_a", "pre_b", "mid_ps", "fin_a", "fin_b"))
        bf = lambda b: b[:].bitcast(BF16)

        names = """x_in x_res stored consts_in w_in consts_ready
            c0 sq0 j0 ln0 rs0 xh0 x1 c1 sq1 j1 ln1 rs1 xh1 xn carry dx mix_w mix_a mix_k mix_v mix_r mix_g
            w1 th_w a1 low_a k key v val r rec g1 th_g0 th_g w2 th_d a2 th_a dec cum p inv_p
            sqk kks nrm lnk rk kk kki b_t a_t ka_f k2 k_t r_t rkb rkb_ps bonus bonus_b g2 gate
            state s_a sa plus_kv upd vb kv s_r o
            o_sb gc gsq gj gln grs gxh gaff gg wo x2 x2x fc fsq fj fln frs fxh xf fcarry fdx kf
            f1 relu hid
            f2 y1 y1b ec esq ej eln ers h router best eq score best2 onehot masks h_e pick_ps pick moe act
            mo y2 lc lsq lj lln lrs lxh res""".split()
        s = {n: sem("s_" + n) for n in names}
        block = ctx.enter_context(nc.Block())

        def bt(ap):
            return ap.rearrange("p (b t) -> p t b", b=B)

        def tb(ap, t=STEPS):
            return ap.rearrange("p (t b) -> p t b", t=t)

        def over_i(ap):
            return ap.unsqueeze(1).broadcast_to([128, N, B])

        def st(n):
            return state[:, n * STATE:(n + 1) * STATE]

        def pipeline(eng, fill, parts, scan_step, finish, before_step=lambda t: None):
            fill()

            def iteration(c):
                stages = [Part(make(c + skew)) for skew, make in parts
                          if (c + skew).has()]
                scanning = c.has()
                for t in range(STEPS):
                    before_step(t)
                    if scanning and scan_step:
                        scan_step(c, t, stages)
                    else:
                        for stage in stages:
                            stage.upto(t)
                for stage in stages:
                    stage.upto(10 ** 5)

            for c in (-1, 0, 1):
                if c < 0:
                    for skew, make in parts:
                        if skew == 1:
                            Part(make(Chunk(0, 0))).upto(10 ** 5)
                else:
                    iteration(Chunk(0, c))
            iteration(Chunk(0, 2))
            loops = (CHUNKS - 1 - RING) // RING
            with eng.Fori(RING, RING * loops + 1, RING) as first:
                for n in range(RING):
                    iteration(Chunk(first, n))
            for c in range(RING + RING * loops, CHUNKS + 2):
                iteration(Chunk(0, c))
            finish()

        last_pre = CHUNKS - 1

        @block.sync
        def _(sp):
            def fill():
                sp.dma_start(con[:], consts).then_inc(s["consts_in"], 16)
                sp.dma_start(vec[:], vecs).then_inc(s["consts_in"], 16)
                sp.dma_start(mat[:], mats).then_inc(s["w_in"], 16)
                sp.dma_start(b1_rows[:], b1_in).then_inc(s["w_in"], 16)

            def pre(c):
                cols, last = c.cols(sp), settled(sp, (c + -1).count()) if c.has(1) else None
                sp.wait_ge(s["consts_in"], 32)
                if c.has(1):
                    sp.wait_ge(s["c0"], last)
                sp.dma_start(x_in[c.slot][:], xT[:, cols]).then_inc(s["x_in"], 16)
                yield 1

            def mid(c):
                cols, last = c.cols(sp), settled(sp, (c + -1).count()) if c.has(1) else None
                sp.wait_ge(s["w_in"], 32)
                if c.has(1):
                    sp.wait_ge(s["x2x"], last)
                sp.dma_start(x_res[c.slot][:], xT[:, cols]).then_inc(s["x_res"], 16)
                yield 1

            def fin(c):
                yield 20
                cols, now = c.cols(sp), settled(sp, c.count())
                sp.wait_ge(s["w_in"], 32)
                sp.wait_ge(s["res"], now)
                sp.dma_start(out[:, cols], res[c.slot][:]).then_inc(s["stored"], 16)
                yield 21

            def finish():
                sp.wait_ge(s["stored"], 16 * CHUNKS)

            pipeline(nc.sync, fill, [(1, pre), (-1, mid), (-2, fin)], None, finish)

        @block.tensor
        def _(pe):
            mm = nc.tensor.matmul

            def one(bank_, lhsT, rhs, name):
                return mm(bank_, lhsT, rhs, start=True, stop=True).then_inc(s[name], 1)

            def fill():
                pe.wait_ge(s["consts_in"], 32)
                pe.wait_ge(s["w_in"], 32)
                pe.wait_ge(s["consts_ready"], 19)

            def spread(c, q, half):
                if half == 0:
                    pe.wait_ge(s["val"], c.count())
                before = c.count(2 * q + half, 2 * QUARTERS)
                if not (isinstance(before, int) and before == 0):
                    pe.wait_ge(s["kv"], before)
                for n in range(N // 2):
                    i = half * N // 2 + n
                    last = mm(vb_ps[:, n * QCOLS:(n + 1) * QCOLS], k("spread", i),
                              val[c.slot][:, q * QCOLS:(q + 1) * QCOLS], start=(n == 0), stop=True,
                              skip_group_check=True)
                last.then_inc(s["vb"], 1)

            def outputs(c, q, half):
                if half == 0:
                    pe.wait_ge(s["s_r"], c.count(4 * q + 4, 4 * QUARTERS))
                    if q == 0 and c.has(1):
                        pe.wait_ge(s["o_sb"], (c + -1).count())
                part = s_r[:, (q % 2) * QUARTER * STATE:(q % 2 + 1) * QUARTER * STATE]
                part = part.rearrange("p (t i b) -> p i t b", t=QUARTER, i=N)
                for n in range(N // 2):
                    i = half * N // 2 + n
                    last = mm(o_ps[:, q * QCOLS:(q + 1) * QCOLS], k("gather", i), part[:, i],
                              start=(i == 0), stop=(i == N - 1), skip_group_check=True)
                if half:
                    last.then_inc(s["o"], 1)

            def scan_step(c, t, stages):
                pe.wait_ge(s["s_a"], c.count(t + 1, STEPS))
                mm(sa_ps[:, 0:STATE], k("sum8"), s_a[:], start=True, stop=True).then_inc(s["sa"], 1)
                q, at = divmod(t, QUARTER)
                nxt = (c, q + 1) if q + 1 < QUARTERS else (c + 1, 0)
                if at in (1, 2) and nxt[0].has():
                    spread(*nxt, at - 1)
                done = (c, q - 1) if q else (c + -1, QUARTERS - 1)
                if at in (3, 4) and done[0].has():
                    outputs(*done, at - 3)
                for stage in stages:
                    stage.upto(t)

            def pre(c):
                pe.wait_ge(s["x_in"], c.count(16, 16))
                back = c + -3
                if c.has(3):
                    pe.wait_ge(s["relu"], back.count(2, J))
                if c.has(1):
                    pe.wait_ge(s["bonus"], (c + -1).count())
                one(pre_a[:], k("center"), x_in[c.slot][:], "c0")
                yield 1
                pe.wait_ge(s["sq0"], c.count())
                if c.has(3):
                    pe.wait_ge(s["relu"], back.count(4, J))
                if c.has(1):
                    pe.wait_ge(s["gate"], (c + -1).count())
                one(pre_b[:], k("mean"), sq_p[:], "j0")
                yield 3
                pe.wait_ge(s["x1"], c.count())
                one(pre_a[:], k("center"), x1[c.slot][:], "c1")
                yield 4
                pe.wait_ge(s["sq1"], c.count())
                pe.wait_ge(s["ln0"], c.count())
                one(pre_b[:], k("mean"), sq_p[:], "j1")
                yield 8
                pe.wait_ge(s["mix_w"], c.count())
                pe.wait_ge(s["xh1"], c.count())
                mm(pre_a[0:DW, :], w("w1", 0, DW), mix["w"][:], start=True, stop=True).then_inc(s["w1"], 1)
                pe.wait_ge(s["mix_k"], c.count())
                pe.wait_ge(s["ln1"], c.count())
                one(pre_b[:], w("W_k"), mix["k"][:], "k")
                yield 9
                pe.wait_ge(s["mix_a"], c.count())
                pe.wait_ge(s["th_w"], c.count())
                mm(pre_a[DW:2 * DW, :], w("a1", 0, DW), mix["a"][:], start=True, stop=True).then_inc(s["a1"], 1)
                yield 10
                pe.wait_ge(s["mix_g"], c.count())
                pe.wait_ge(s["key"], c.count())
                one(pre_b[:], w("g1"), mix["g"][:], "g1")
                yield 11
                pe.wait_ge(s["th_w"], c.count())
                pe.wait_ge(s["low_a"], c.count())
                one(pre_a[:], w("w2_a2")[0:DW, :], th_w, "w2")
                yield 12
                pe.wait_ge(s["low_a"], c.count())
                pe.wait_ge(s["th_g0"], c.count())
                one(pre_b[:], w("w2_a2")[DW:2 * DW, :], low_a, "a2")
                yield 13
                pe.wait_ge(s["mix_v"], c.count())
                pe.wait_ge(s["th_d"], c.count())
                one(pre_a[:], w("W_v"), mix["v"][:], "v")
                yield 14
                pe.wait_ge(s["sqk"], c.count())
                pe.wait_ge(s["th_a"], c.count())
                one(pre_b[:], k("sum8"), sq_p[:], "kks")
                yield 15
                pe.wait_ge(s["mix_r"], c.count())
                pe.wait_ge(s["val"], c.count())
                one(pre_a[:], w("W_r"), mix["r"][:], "r")
                yield 16
                pe.wait_ge(s["th_g"], c.count())
                pe.wait_ge(s["nrm"], c.count())
                one(pre_b[:], w("g2"), th_g[:], "g2")
                yield 21
                pe.wait_ge(s["rkb"], c.count())
                pe.wait_ge(s["rec"], c.count())
                one(pre_a[:], k("sum8"), rkb[:], "rkb_ps")
                yield 22

            def mid(c):
                if isinstance(c.base, int) and c.off == CHUNKS - 1:
                    outputs(c, QUARTERS - 1, 0)
                    outputs(c, QUARTERS - 1, 1)
                yield 6
                pe.wait_ge(s["o_sb"], c.count())
                if c.has(1):
                    pe.wait_ge(s["y1"], (c + -1).count())
                one(mid_ps[:], k("center8"), o_sb[:], "gc")
                yield 7
                pe.wait_ge(s["gsq"], c.count())
                pe.wait_ge(s["kv"], vb_free(c, 1))
                one(vb_ps[:], k("mean8"), sq_m[:], "gj")
                yield 8
                pe.wait_ge(s["gln"], c.count())
                yield 13
                pe.wait_ge(s["gg"], c.count())
                one(mid_ps[:], w("W_o"), z_m[:], "wo")
                yield 15
                pe.wait_ge(s["x2"], c.count())
                one(mid_ps[:], k("center"), x2[:], "fc")
                yield 21
                pe.wait_ge(s["fsq"], c.count())
                pe.wait_ge(s["kv"], vb_free(c, 3))
                one(vb_ps[:], k("mean"), sq_m[:], "fj")
                yield 24
                pe.wait_ge(s["fln"], c.count())
                yield 27
                pe.wait_ge(s["kf"], c.count())
                for j in range(J):
                    if j == 1:
                        pe.wait_ge(s["bonus"], newest_pre(c))
                    if j == 2:
                        pe.wait_ge(s["relu"], c.count(1, J))
                    if j == 3:
                        pe.wait_ge(s["gate"], newest_pre(c))
                    to = (mid_ps, pre_a, mid_ps, pre_b)[j]
                    one(to[:], w("ffn1", j), kf[:], "f1")
                    yield 28 + j

            def vb_free(c, quarters):
                if isinstance(c.base, int) and c.off == CHUNKS - 1:
                    return CHUNKS * 2 * QUARTERS
                n = (c + 1).count(2 * quarters + 2, 2 * QUARTERS)
                if isinstance(c.base, int):
                    n = min(n, CHUNKS * 2 * QUARTERS)
                return n

            def newest_pre(c):
                if isinstance(c.base, int):
                    return min((c + 2).count(), CHUNKS)
                return (c + 2).count()

            def fin(c):
                for j in range(J):
                    pe.wait_ge(s["hid"], c.count(j + 1, J))
                    if j == 0:
                        pe.wait_ge(s["relu"], c.count(3, J))
                    last = mm(mid_ps[:], w("ffn2", j), hid[j][:], start=(j == 0), stop=(j == J - 1))
                    if j == 1:
                        yield 1
                last.then_inc(s["f2"], 1)
                yield 3
                pe.wait_ge(s["y1"], c.count())
                if c.has(1):
                    pe.wait_ge(s["lln"], (c + -1).count())
                one(fin_a[:], k("center"), y1[:], "ec")
                yield 4
                pe.wait_ge(s["esq"], c.count())
                if c.has(1):
                    pe.wait_ge(s["lxh"], (c + -1).count())
                one(fin_b[:], k("mean"), sq_f[:], "ej")
                yield 6
                pe.wait_ge(s["h"], c.count())
                for n in range(4):
                    last = mm(fin_a[:, n * E:(n + 1) * E], h[:, n * C:(n + 1) * C], w("router", 0, E),
                              start=(n == 0), stop=True, skip_group_check=True)
                last.then_inc(s["router"], 1)
                yield 9
                pe.wait_ge(s["onehot"], c.count())
                pe.wait_ge(s["eln"], c.count())
                for e in range(E):
                    to = bf(fin_b if e < 2 else fin_a)
                    for n in range(4):
                        last = nc.tensor.transpose(
                            to[:, (e % 2) * COLS + n * C:(e % 2) * COLS + (n + 1) * C],
                            onehot[:, n * E + e:n * E + e + 1].broadcast_to([128, C]), ident_bf[:])
                    if e % 2:
                        last.then_inc(s["masks"], 1)
                yield 10
                pe.wait_ge(s["h_e"], c.count(2, E))
                for n in range(4):
                    last = nc.tensor.transpose(bf(fin_b)[0:E, n * C:(n + 1) * C],
                                               onehot[:, n * E:(n + 1) * E], ident_bf[:])
                last.then_inc(s["pick_ps"], 1)
                for j in range(J):
                    to = (fin_a, fin_b)[j % 2]
                    if j >= 2:
                        pe.wait_ge(s["act"], c.count(j - 1, J))
                    for e in range(E):
                        if j == 0:
                            pe.wait_ge(s["h_e"], c.count(4 if e == 0 else e + 1, E))
                        mm(to[:], mat[:, M["W1"] + e * I + j * C:M["W1"] + e * I + (j + 1) * C],
                           h_e[e][:], start=(e == 0), stop=False)
                        if e == 1:
                            yield 11 + 2 * j
                    pe.wait_ge(s["pick"], c.count())
                    for n in range(3):
                        last = mm(to[:], b1_parts[n][:, j * C:(j + 1) * C], pick[:], start=False, stop=(n == 2))
                    last.then_inc(s["moe"], 1)
                    yield 12 + 2 * j
                yield 18
                for j in range(J):
                    pe.wait_ge(s["act"], c.count(max(j + 1, 3), J))
                    last = mm(fin_a[:], w("Wo", j), act_j[j][:], start=(j == 0), stop=(j == J - 1))
                    if j == 1:
                        yield 19
                last.then_inc(s["mo"], 1)
                yield 20
                pe.wait_ge(s["y2"], c.count())
                one(fin_b[:], k("center"), y2[:], "lc")
                yield 21
                pe.wait_ge(s["lsq"], c.count())
                one(fin_a[:], k("mean"), sq_f[:], "lj")
                yield 22

            def first_quarter(c):
                yield from pre(c)
                if isinstance(c.base, int) and c.off == 0:
                    spread(c, 0, 0)
                    spread(c, 0, 1)

            pipeline(nc.tensor, fill, [(1, first_quarter), (-1, mid), (-2, fin)], scan_step, lambda: None)

        @block.scalar
        def _(act):
            f = nc.scalar.activation

            def fill():
                act.wait_ge(s["consts_in"], 32)
                act.wait_ge(s["consts_ready"], 19)
                nc.scalar.preload_act_table_set("natural_log_exp_and_others")

            def rsqrt(c, var, eps, lv, rs, n_in, n_ln, n_rs, scale=1.0):
                act.wait_ge(s[n_in], c.count())
                f(lv, var, ACT.Ln, bias=eps, scale=scale).then_inc(s[n_ln], 1)
                act.wait_ge(s[n_ln], c.count())
                f(rs, lv, ACT.Exp, scale=-0.5).then_inc(s[n_rs], 1)

            def pre(c):
                act.wait_ge(s["c0"], c.count())
                if c.has(1):
                    act.wait_ge(s["kks"], (c + -1).count())
                f(sq_p[:], pre_a[:], ACT.Square).then_inc(s["sq0"], 1)
                yield 1
                if c.has(1):
                    act.wait_ge(s["kk"], (c + -1).count())
                rsqrt(c, pre_b[:], eps_sq, lv_p[:], rs_p[:], "j0", "ln0", "rs0", scale=1.0 + 1e-5)
                yield 3
                act.wait_ge(s["c1"], c.count())
                act.wait_ge(s["j0"], c.count())
                f(sq_p[:], pre_a[:], ACT.Square).then_inc(s["sq1"], 1)
                if c.has(1):
                    act.wait_ge(s["xn"], (c + -1).count())
                    act.wait_ge(s["mix_r"], (c + -1).count())
                    f(xn[c.slot][:, 0:B], xn[c.slot][:, COLS:COLS + B], ACT.Identity).then_inc(s["carry"], 1)
                yield 4
                act.wait_ge(s["xh0"], c.count())
                rsqrt(c, pre_b[:], eps_ln, lv_p[:], rs_p[:], "j1", "ln1", "rs1")
                yield 9
                act.wait_ge(s["k"], c.count())
                if c.has(1):
                    act.wait_ge(s["k2"], (c + -1).count())
                    act.wait_ge(s["kk"], (c + -1).count())
                f(key[:], pre_b[:], ACT.Identity).then_inc(s["key"], 1)
                act.wait_ge(s["w1"], c.count())
                if c.has(1):
                    act.wait_ge(s["w2"], (c + -1).count())
                f(th_w, pre_a[0:DW, :], ACT.Tanh).then_inc(s["th_w"], 1)
                yield 10
                act.wait_ge(s["a1"], c.count())
                if c.has(1):
                    act.wait_ge(s["a2"], (c + -1).count())
                f(low_a, pre_a[DW:2 * DW, :], ACT.Identity).then_inc(s["low_a"], 1)
                yield 11
                act.wait_ge(s["g1"], c.count())
                if c.has(1):
                    act.wait_ge(s["g2"], (c + -1).count())
                f(th_g[:], pre_b[:], ACT.Tanh, scale=0.5).then_inc(s["th_g0"], 1)
                yield 12
                act.wait_ge(s["w2"], c.count())
                if c.has(1):
                    act.wait_ge(s["k_t"], (c + -1).count())
                    act.wait_ge(s["kki"], (c + -1).count())
                f(bt(dec_bt[:]), tb(pre_a[:]), ACT.Tanh, bias=half_w0[:], scale=0.5).then_inc(s["th_d"], 1)
                act.wait_ge(s["key"], c.count())
                act.wait_ge(s["j1"], c.count())
                f(sq_p[:], key[:], ACT.Square, scale=v("k_k")).then_inc(s["sqk"], 1)
                yield 13
                act.wait_ge(s["a2"], c.count())
                if c.has(1):
                    act.wait_ge(s["b_t"], (c + -1).count())
                    act.wait_ge(s["ka_f"], (c + -1).count())
                act.wait_ge(s["mix_r"], c.count())
                f(th_a[:], pre_b[:], ACT.Tanh, bias=half_a0[:], scale=0.5).then_inc(s["th_a"], 1)
                yield 14
                act.wait_ge(s["v"], c.count())
                f(val[c.slot][:], pre_a[:], ACT.Identity).then_inc(s["val"], 1)
                yield 16
                act.wait_ge(s["r"], c.count())
                act.wait_ge(s["xn"], c.count())
                f(rec[:], pre_a[:], ACT.Identity).then_inc(s["rec"], 1)
                yield 17
                act.wait_ge(s["g2"], c.count())
                f(gate[c.slot][:], pre_b[:], ACT.Identity).then_inc(s["gate"], 1)
                yield 19
                act.wait_ge(s["cum"], c.count())
                f(tb(p_all[c.slot][:, B:B + COLS]), bt(cum_bt[:]), ACT.Exp, scale=-DECAY).then_inc(s["p"], 1)
                f(tb(inv_p[:]), bt(cum_bt[:]), ACT.Exp, scale=DECAY).then_inc(s["inv_p"], 1)
                act.wait_ge(s["xh1"], c.count())
                rsqrt(c, lv_p[:], 0.0, lv_p[:], rs_p[:], "nrm", "lnk", "rk")
                yield 20

            def mid(c):
                yield 5
                act.wait_ge(s["o"], c.count(QUARTERS, QUARTERS))
                if c.has(1):
                    act.wait_ge(s["fc"], (c + -1).count())
                    act.wait_ge(s["x2x"], (c + -1).count())
                f(o_sb[:], o_ps[:], ACT.Identity).then_inc(s["o_sb"], 1)
                yield 6
                act.wait_ge(s["gc"], c.count())
                if c.has(1):
                    act.wait_ge(s["fj"], (c + -1).count())
                f(sq_m[:], mid_ps[:], ACT.Square).then_inc(s["gsq"], 1)
                yield 7
                if c.has(1):
                    act.wait_ge(s["fxh"], (c + -1).count())
                rsqrt(c, vb_ps[:], eps_gn, rs_m[:], rs_m[:], "gj", "gln", "grs")
                yield 20
                act.wait_ge(s["fc"], c.count())
                act.wait_ge(s["gj"], c.count())
                f(sq_m[:], mid_ps[:], ACT.Square).then_inc(s["fsq"], 1)
                if c.has(1):
                    act.wait_ge(s["xf"], (c + -1).count())
                    act.wait_ge(s["kf"], (c + -1).count())
                    f(xf[c.slot][:, 0:B], xf[c.slot][:, COLS:COLS + B], ACT.Identity).then_inc(s["fcarry"], 1)
                yield 22
                act.wait_ge(s["gxh"], c.count())
                rsqrt(c, vb_ps[:], eps_ln, rs_m[:], rs_m[:], "fj", "fln", "frs")
                yield 28
                for j in range(J):
                    act.wait_ge(s["f1"], c.count(j + 1, J))
                    if j == 0 and c.has(1):
                        act.wait_ge(s["mo"], (c + -1).count())
                    f(hid[j][:], (mid_ps, pre_a, mid_ps, pre_b)[j][:], ACT.Relu).then_inc(s["relu"], 1)
                    act.wait_ge(s["relu"], c.count(j + 1, J))
                    f(hid[j][:], hid[j][:], ACT.Square).then_inc(s["hid"], 1)
                    yield 29 + j

            def fin(c):
                yield 3
                act.wait_ge(s["ec"], c.count())
                if c.has(1):
                    act.wait_ge(s["lj"], (c + -1).count())
                f(sq_f[:], fin_a[:], ACT.Square).then_inc(s["esq"], 1)
                yield 4
                if c.has(1):
                    act.wait_ge(s["lxh"], (c + -1).count())
                rsqrt(c, fin_b[:], eps_ln, rs_f[:], rs_f[:], "ej", "eln", "ers")
                yield 10
                act.wait_ge(s["pick_ps"], c.count())
                f(pick[:], bf(fin_b)[0:E, 0:COLS], ACT.Identity).then_inc(s["pick"], 1)
                yield 11
                for j in range(J):
                    act.wait_ge(s["moe"], c.count(j + 1, J))
                    if j == 0:
                        act.wait_ge(s["f2"], c.count())
                    f(act_j[j][:], (fin_a, fin_b)[j % 2][:], ACT.Gelu).then_inc(s["act"], 1)
                    yield 13 + 2 * j
                yield 21
                act.wait_ge(s["lc"], c.count())
                act.wait_ge(s["ej"], c.count())
                f(sq_f[:], fin_b[:], ACT.Square).then_inc(s["lsq"], 1)
                yield 22
                act.wait_ge(s["h"], c.count())
                rsqrt(c, fin_a[:], eps_last, rs_f[:], rs_f[:], "lj", "lln", "lrs")
                yield 23

            def tables(t):
                if t in (0, 18):
                    nc.scalar.preload_act_table_set("natural_log_exp_and_others")
                if t == 9:
                    nc.scalar.preload_act_table_set("gelu_and_others")

            pipeline(nc.scalar, fill, [(1, pre), (-1, mid), (-2, fin)], None, lambda: None, tables)

        @block.vector
        def _(dve):
            tt, ts, stt = nc.vector.tensor_tensor, nc.vector.tensor_scalar, nc.vector.scalar_tensor_tensor
            made = [0]

            def const(op):
                op.then_inc(s["consts_ready"], 1)
                made[0] += 1
                dve.wait_ge(s["consts_ready"], made[0])

            def fill():
                dve.wait_ge(s["consts_in"], 32)
                const(nc.vector.tensor_copy(ident_bf[:], k("ident")))
                const(ts(half_w0[:], v("w0"), 0.5, None, ALU.mult))
                const(ts(half_a0[:], v("a0"), 0.5, None, ALU.mult))
                const(ts(half_ka[:], v("k_a"), 0.5, None, ALU.mult))
                const(ts(rest_ka[:], half_ka[:], -1.0, 1.0, ALU.mult, ALU.add))
                const(nc.vector.memset(scan_keep[:], 1.0))
                const(nc.vector.memset(bt(scan_keep[:])[:, 0, :], 0.0))
                for value, tile in eps.items():
                    const(nc.vector.memset(tile[:], value))
                for n in range(RING):
                    const(nc.vector.memset(p_all[n][:, 0:B], 1.0))
                dve.wait_ge(s["w_in"], 32)
                const(nc.vector.tensor_copy(b1_parts[0][:], b1_rows[:]))
                const(tt(b1_rest[:], b1_rows[:], b1_parts[0][:], ALU.subtract))
                const(nc.vector.tensor_copy(b1_parts[1][:], b1_rest[:]))
                const(tt(b1_rest[:], b1_rest[:], b1_parts[1][:], ALU.subtract))
                const(nc.vector.tensor_copy(b1_parts[2][:], b1_rest[:]))
                nc.vector.memset(st(0), 0.0).then_inc(s["state"], 1)

            def ib(ap):
                return ap.rearrange("p (i b) -> p i b", i=N)

            def spread_kv(c, q, half):
                if half == 0:
                    dve.wait_ge(s["k_t"], c.count())
                dve.wait_ge(s["vb"], c.count(2 * q + half + 1, 2 * QUARTERS))
                part = kv[:, (q % 2) * QUARTER * STATE:(q % 2 + 1) * QUARTER * STATE]
                part = part.rearrange("p (t i b) -> p i t b", t=QUARTER, i=N)[:, half * 4:half * 4 + 4]
                keys = k_t[c.slot][:, q * QCOLS:(q + 1) * QCOLS].rearrange("p (t b) -> p t b", t=QUARTER)
                tt(part, vb_ps[:].rearrange("p (i t b) -> p i t b", i=N // 2, t=QUARTER),
                   keys.unsqueeze(1).broadcast_to([128, N // 2, QUARTER, B]), ALU.mult).then_inc(s["kv"], 1)

            def scan_step(c, t, stages):
                if t == 0 and c.has(1):
                    dve.wait_ge(s["state"], c.count(0, STEPS + 1))
                    last = p_all[(c + -1).slot][:, COLS:COLS + B]
                    tt(ib(st(0)), ib(st(STEPS)), over_i(last), ALU.mult).then_inc(s["state"], 1)
                if t == 0:
                    dve.wait_ge(s["a_t"], c.count())
                dve.wait_ge(s["state"], c.count(t + 1, STEPS + 1))
                tt(ib(s_a[:]), ib(st(t)), over_i(a_t[c.slot][:, t * B:(t + 1) * B]), ALU.mult).then_inc(s["s_a"], 1)
                q, at = divmod(t, QUARTER)
                nxt = (c, q + 1) if q + 1 < QUARTERS else (c + 1, 0)
                if at in (2, 3) and nxt[0].has():
                    spread_kv(*nxt, at - 2)
                for stage in stages:
                    stage.upto(t)
                if t == 0:
                    dve.wait_ge(s["b_t"], c.count())
                dve.wait_ge(s["sa"], c.count(t + 1, STEPS))
                tt(ib(upd[:]), ib(sa_ps[:, 0:STATE]), over_i(b_t[c.slot][:, t * B:(t + 1) * B]),
                   ALU.mult).then_inc(s["upd"], 1)
                dve.wait_ge(s["upd"], c.count(t + 1, STEPS))
                dve.wait_ge(s["plus_kv"], c.count(t + 1, STEPS))
                tt(st(t + 1), upd[:], plus_kv[:, (t % 2) * STATE:(t % 2 + 1) * STATE], ALU.add).then_inc(s["state"], 1)

            def pre(c):
                yield 2
                dve.wait_ge(s["rs0"], c.count())
                if c.has(1):
                    dve.wait_ge(s["r_t"], (c + -1).count())
                    dve.wait_ge(s["rkb"], (c + -1).count())
                tt(xh_p[:], pre_a[:], rs_p[:], ALU.mult).then_inc(s["xh0"], 1)
                yield 5
                dve.wait_ge(s["rs1"], c.count())
                dve.wait_ge(s["x1"], c.count())
                tt(xh_p[:], pre_a[:], rs_p[:], ALU.mult).then_inc(s["xh1"], 1)
                yield 6
                dve.wait_ge(s["xn"], c.count())
                dve.wait_ge(s["carry"], c.count())
                if c.has(1):
                    dve.wait_ge(s["b_t"], (c + -1).count())
                    dve.wait_ge(s["ka_f"], (c + -1).count())
                now = xn[c.slot][:, B:B + COLS]
                tt(dx[:], xn[c.slot][:, 0:COLS], now, ALU.subtract).then_inc(s["dx"], 1)
                yield 7
                dve.wait_ge(s["dx"], c.count())
                for q, read, at in (("w", "rkb_ps", 7), ("k", "r", 8), ("a", "a_t", 8), ("g", "b_t", 9),
                                    ("v", "w1", 10), ("r", "k", 11)):
                    if q in "vr":
                        dve.wait_ge(s[read], c.count())
                    elif c.has(1):
                        dve.wait_ge(s[read], (c + -1).count())
                    stt(mix[q][:], dx[:], v("x_" + q), now, ALU.mult, ALU.add).then_inc(s["mix_" + q], 1)
                    yield at
                yield 12
                dve.wait_ge(s["th_d"], c.count())
                ts(dec_bt[:], dec_bt[:], 0.5, 0.5, ALU.mult, ALU.add).then_inc(s["dec"], 1)
                yield 13
                dve.wait_ge(s["dec"], c.count())
                if c.has(1):
                    dve.wait_ge(s["inv_p"], (c + -1).count())
                nc.vector.tensor_tensor_scan(cum_bt[:], scan_keep[:], dec_bt[:], 0.0,
                                             ALU.mult, ALU.add).then_inc(s["cum"], 1)
                yield 15
                dve.wait_ge(s["kks"], c.count())
                dve.wait_ge(s["rs1"], c.count())
                ts(lv_p[:], pre_b[:], 1e-24, None, ALU.max).then_inc(s["nrm"], 1)
                yield 18
                dve.wait_ge(s["rec"], c.count())
                dve.wait_ge(s["k2"], c.count())
                dve.wait_ge(s["v"], c.count())
                stt(rkb[:], rec[:], v("r_k"), k2[:], ALU.mult, ALU.mult).then_inc(s["rkb"], 1)
                yield 20
                dve.wait_ge(s["rk"], c.count())
                dve.wait_ge(s["key"], c.count())
                stt(kk[:], key[:], v("k_k"), rs_p[:], ALU.mult, ALU.mult).then_inc(s["kk"], 1)
                dve.wait_ge(s["inv_p"], c.count())
                tt(k_t[c.slot][:], k2[:], inv_p[:], ALU.mult).then_inc(s["k_t"], 1)
                yield 21
                dve.wait_ge(s["kk"], c.count())
                stt(kki[:], kk[:], 0.5, inv_p[:], ALU.mult, ALU.mult).then_inc(s["kki"], 1)
                dve.wait_ge(s["p"], c.count())
                stt(a_t[c.slot][:], kk[:], -1.0, p_all[c.slot][:, 0:COLS], ALU.mult, ALU.mult).then_inc(s["a_t"], 1)
                yield 22
                dve.wait_ge(s["kki"], c.count())
                dve.wait_ge(s["th_a"], c.count())
                stt(b_t[c.slot][:], th_a[:], 1.0, kki[:], ALU.add, ALU.mult).then_inc(s["b_t"], 1)
                dve.wait_ge(s["rkb_ps"], c.count())
                dve.wait_ge(s["val"], c.count())
                tt(bonus[c.slot][:], pre_a[:], val[c.slot][:], ALU.mult).then_inc(s["bonus"], 1)
                yield 23

            def mid(c):
                yield 9
                dve.wait_ge(s["grs"], c.count())
                tt(y_m[:], mid_ps[:], rs_m[:], ALU.mult).then_inc(s["gxh"], 1)
                yield 10
                dve.wait_ge(s["gxh"], c.count())
                dve.wait_ge(s["bonus_b"], c.count())
                if c.has(1):
                    dve.wait_ge(s["f1"], c.count(0, J))
                stt(z_m[:], y_m[:], v("gn_w"), bonus[c.slot][:], ALU.mult, ALU.add).then_inc(s["gaff"], 1)
                yield 11
                dve.wait_ge(s["gaff"], c.count())
                dve.wait_ge(s["gate"], c.count())
                tt(z_m[:], z_m[:], gate[c.slot][:], ALU.mult).then_inc(s["gg"], 1)
                yield 14
                dve.wait_ge(s["wo"], c.count())
                dve.wait_ge(s["x1"], c.count())
                if c.has(1):
                    dve.wait_ge(s["gc"], c.count())
                tt(x2[:], mid_ps[:], x1[c.slot][:], ALU.add).then_inc(s["x2"], 1)
                yield 23
                dve.wait_ge(s["frs"], c.count())
                tt(y_m[:], mid_ps[:], rs_m[:], ALU.mult).then_inc(s["fxh"], 1)
                yield 25
                dve.wait_ge(s["xf"], c.count())
                dve.wait_ge(s["fcarry"], c.count())
                now = xf[c.slot][:, B:B + COLS]
                tt(y_m[:], xf[c.slot][:, 0:COLS], now, ALU.subtract).then_inc(s["fdx"], 1)
                yield 26
                dve.wait_ge(s["fdx"], c.count())
                dve.wait_ge(s["wo"], c.count())
                stt(kf[:], y_m[:], v("ffn_x_k"), now, ALU.mult, ALU.add).then_inc(s["kf"], 1)
                yield 27

            def fin(c):
                yield 2
                dve.wait_ge(s["f2"], c.count())
                dve.wait_ge(s["x2x"], c.count())
                if c.has(1):
                    dve.wait_ge(s["ec"], (c + -1).count())
                    dve.wait_ge(s["y1b"], (c + -1).count())
                tt(y1[:], mid_ps[:], x2x[c.slot][:], ALU.add).then_inc(s["y1"], 1)
                yield 5
                dve.wait_ge(s["ers"], c.count())
                if c.has(1):
                    dve.wait_ge(s["y2"], (c + -1).count())
                tt(h[:], fin_a[:], rs_f[:], ALU.mult).then_inc(s["h"], 1)
                yield 7
                dve.wait_ge(s["router"], c.count())
                logits = fin_a[:, 0:4 * E].rearrange("p (n e) -> p n e", e=E)
                rows = lambda a: a[:].rearrange("p (n e) -> p n e", e=E)
                every = lambda a: a[:].unsqueeze(2).broadcast_to([128, 4, E])
                nc.vector.tensor_reduce(best[:], logits, AX.X, ALU.max).then_inc(s["best"], 1)
                dve.wait_ge(s["best"], c.count())
                tt(rows(eq), logits, every(best), ALU.is_ge).then_inc(s["eq"], 1)
                dve.wait_ge(s["eq"], c.count())
                tt(score[:], eq[:], k("rank", 0, 4 * E), ALU.mult).then_inc(s["score"], 1)
                yield 8
                dve.wait_ge(s["score"], c.count())
                nc.vector.tensor_reduce(best2[:], rows(score), AX.X, ALU.max).then_inc(s["best2"], 1)
                dve.wait_ge(s["best2"], c.count())
                if c.has(1):
                    dve.wait_ge(s["pick_ps"], (c + -1).count())
                tt(rows(onehot), rows(score), every(best2), ALU.is_equal).then_inc(s["onehot"], 1)
                yield 9
                for e in range(E):
                    dve.wait_ge(s["masks"], c.count(e // 2 + 1, 2))
                    if e == 0 and c.has(1):
                        dve.wait_ge(s["res"], (c + -1).count())
                        dve.wait_ge(s["moe"], c.count(0, J))
                    mask = bf(fin_b if e < 2 else fin_a)[:, (e % 2) * COLS:(e % 2 + 1) * COLS]
                    tt(h_e[e][:], mask, h[:], ALU.mult).then_inc(s["h_e"], 1)
                    if e == 1:
                        yield 10
                yield 20
                dve.wait_ge(s["mo"], c.count())
                stt(y2[:], fin_a[:], v("bo"), h[:], ALU.add, ALU.add).then_inc(s["y2"], 1)
                yield 23
                dve.wait_ge(s["lrs"], c.count())
                tt(y2[:], fin_b[:], rs_f[:], ALU.mult).then_inc(s["lxh"], 1)
                yield 24
                dve.wait_ge(s["lxh"], c.count())
                dve.wait_ge(s["y1b"], c.count())
                if c.has(1):
                    dve.wait_ge(s["stored"], (c + -1).count(16, 16))
                stt(res[c.slot][:], y2[:], v("ln_gamma"), y1b[:], ALU.mult, ALU.add).then_inc(s["res"], 1)
                yield 25

            def first_quarter(c):
                yield from pre(c)
                if isinstance(c.base, int) and c.off == 0:
                    spread_kv(c, 0, 0)
                    spread_kv(c, 0, 1)

            pipeline(nc.vector, fill, [(1, first_quarter), (-1, mid), (-2, fin)], scan_step, lambda: None)

        @block.gpsimd
        def _(pool):
            tt, ts = nc.gpsimd.tensor_tensor, nc.gpsimd.tensor_scalar

            def fill():
                pool.wait_ge(s["consts_in"], 32)
                pool.wait_ge(s["consts_ready"], 19)
                nc.gpsimd.memset(xn[0][:, 0:B], 0.0).then_inc(s["carry"], 1)
                nc.gpsimd.memset(xf[0][:, 0:B], 0.0).then_inc(s["fcarry"], 1)

            def read_out(c, n):
                q, at = divmod(2 * n, QUARTER)
                if at == 0:
                    if n == 0:
                        pool.wait_ge(s["r_t"], c.count())
                    before = c.count(q - 1, QUARTERS)
                    if not isinstance(before, int) or before > 0:
                        pool.wait_ge(s["o"], before)
                first = (q % 2) * QUARTER * STATE + at * STATE
                part = s_r[:, first:first + 2 * STATE].rearrange("p (t i b) -> p t i b", t=2, i=N)
                states = state[:, (2 * n + 1) * STATE:(2 * n + 3) * STATE].rearrange("p (t i b) -> p t i b", t=2, i=N)
                r = r_t[c.slot][:, 2 * n * B:(2 * n + 2) * B].rearrange("p (t b) -> p t b", t=2)
                tt(part, states, r.unsqueeze(2).broadcast_to([128, 2, N, B]), ALU.mult).then_inc(s["s_r"], 1)

            def scan_step(c, t, stages):
                if t % QUARTER == 0:
                    pool.wait_ge(s["kv"], c.count(2 * (t // QUARTER) + 2, 2 * QUARTERS))
                pool.wait_ge(s["state"], c.count(t + 1, STEPS + 1))
                at = (t % (2 * QUARTER)) * STATE
                tt(plus_kv[:, (t % 2) * STATE:(t % 2 + 1) * STATE], st(t), kv[:, at:at + STATE],
                   ALU.add).then_inc(s["plus_kv"], 1)
                if t == 0 and c.has(1):
                    read_out(c + -1, STEPS // 2 - 1)
                if t and t % 2 == 0:
                    read_out(c, t // 2 - 1)
                for stage in stages:
                    stage.upto(t)

            def pre(c):
                now = settled(pool, c.count())
                last = settled(pool, (c + -1).count()) if c.has(1) else None
                yield 2
                pool.wait_ge(s["consts_in"], 32)
                pool.wait_ge(s["xh0"], now)
                ts(x1[c.slot][:], xh_p[:], v("ln_pre_w"), v("ln_pre_b"), ALU.mult, ALU.add).then_inc(s["x1"], 1)
                yield 5
                pool.wait_ge(s["consts_in"], 32)
                pool.wait_ge(s["carry"], now)
                pool.wait_ge(s["xh1"], now)
                ts(xn[c.slot][:, B:B + COLS], xh_p[:], v("ln_attn_w"), v("ln_attn_b"),
                   ALU.mult, ALU.add).then_inc(s["xn"], 1)
                yield 11
                pool.wait_ge(s["consts_in"], 32)
                pool.wait_ge(s["th_g0"], now)
                ts(th_g[:], th_g[:], 0.5, 0.5, ALU.mult, ALU.add).then_inc(s["th_g"], 1)
                yield 14
                pool.wait_ge(s["consts_in"], 32)
                pool.wait_ge(s["th_a"], now)
                if c.has(1):
                    pool.wait_ge(s["k_t"], last)
                    pool.wait_ge(s["rkb"], last)
                ts(k2[:], th_a[:], half_ka[:], rest_ka[:], ALU.mult, ALU.add).then_inc(s["ka_f"], 1)
                yield 15
                pool.wait_ge(s["ka_f"], now)
                pool.wait_ge(s["key"], now)
                tt(k2[:], key[:], k2[:], ALU.mult).then_inc(s["k2"], 1)
                yield 21
                pool.wait_ge(s["p"], now)
                pool.wait_ge(s["rec"], now)
                tt(r_t[c.slot][:], rec[:], p_all[c.slot][:, B:B + COLS], ALU.mult).then_inc(s["r_t"], 1)
                yield 23
                pool.wait_ge(s["consts_in"], 32)
                pool.wait_ge(s["bonus"], now)
                ts(bonus[c.slot][:], bonus[c.slot][:], 1.0, v("gn_b"), ALU.mult, ALU.add).then_inc(s["bonus_b"], 1)
                yield 24

            def mid(c):
                now = settled(pool, c.count())
                last = settled(pool, (c + -1).count()) if c.has(1) else None
                if isinstance(c.base, int) and c.off == CHUNKS - 1:
                    pool.wait_ge(s["state"], CHUNKS * (STEPS + 1))
                    read_out(c, STEPS // 2 - 1)
                yield 15
                pool.wait_ge(s["x2"], now)
                pool.wait_ge(s["x_res"], c.count(16, 16))
                if c.has(1):
                    pool.wait_ge(s["y1"], last)
                tt(x2x[c.slot][:], x2[:], x_res[c.slot][:], ALU.add).then_inc(s["x2x"], 1)
                yield 24
                pool.wait_ge(s["consts_in"], 32)
                pool.wait_ge(s["fcarry"], now)
                pool.wait_ge(s["fxh"], now)
                ts(xf[c.slot][:, B:B + COLS], y_m[:], v("ln_ffn_w"), v("ln_ffn_b"),
                   ALU.mult, ALU.add).then_inc(s["xf"], 1)
                yield 25

            def fin(c):
                now = settled(pool, c.count())
                last = settled(pool, (c + -1).count()) if c.has(1) else None
                yield 3
                pool.wait_ge(s["consts_in"], 32)
                pool.wait_ge(s["y1"], now)
                if c.has(1):
                    pool.wait_ge(s["res"], last)
                ts(y1b[:], y1[:], 1.0, v("ln_beta"), ALU.mult, ALU.add).then_inc(s["y1b"], 1)
                yield 4

            pipeline(nc.gpsimd, fill, [(1, pre), (-1, mid), (-2, fin)], scan_step, lambda: None)


def constants():
    eye = np.eye(C, dtype=np.float32)
    head = np.kron(np.eye(H, dtype=np.float32), np.ones((N, N), np.float32))
    parts = {"center": eye - 1.0 / C, "mean": np.full((C, C), 1.0 / C), "center8": eye - head / N,
             "mean8": head / N, "sum8": head, "ident": eye,
             "rank": np.tile(np.arange(E, 0, -1, dtype=np.float32), (128, 4))}
    spread, gather = [], []
    for i in range(N):
        to_i = np.kron(np.eye(H, dtype=np.float32), np.tile(np.eye(N, dtype=np.float32)[i], (N, 1)))
        gather.append(to_i)
        spread.append(to_i.T)
    parts["spread"], parts["gather"] = np.concatenate(spread, 1), np.concatenate(gather, 1)
    return np.ascontiguousarray(np.concatenate([parts[name] for name in K], 1).astype(np.float32))


def kernel(**inputs):
    import concourse.bacc as bacc
    from concourse.bass_utils import run_bass_kernel_spmd

    a = {name: np.asarray(value) for name, value in inputs.items()}
    attn = lambda name: a["L0_attn_" + name]
    blocks = lambda m: m.reshape(J, C, C).transpose(1, 0, 2).reshape(C, J * C)
    mats = np.concatenate([
        attn("W_k"), attn("w1"), attn("a1"), attn("W_v"), attn("W_r"), attn("g1"), attn("g2"), attn("W_o"),
        np.concatenate([attn("w2"), attn("a2")], 0),
        attn("W_ffn1"), blocks(attn("W_ffn2")), a["L0_ffn_W_router"],
        a["L0_ffn_W1"].transpose(1, 0, 2).reshape(C, E * I), blocks(a["L0_ffn_Wo"])], 1)
    vecs = np.stack([attn(name).reshape(C) for name in VECS] + [a["L0_ffn_" + name] for name in FFN_VECS], 1)
    arrays = {
        "xT": attn("x").transpose(2, 1, 0).reshape(C, T * B),
        "mats": mats,
        "vecs": vecs,
        "consts": constants(),
        "b1": a["L0_ffn_b1"],
    }
    arrays = {name: np.ascontiguousarray(value) for name, value in arrays.items()}
    nc = bacc.Bacc("TRN2", target_bir_lowering=False, num_devices=1)
    aps = [nc.dram_tensor(name, value.shape, F32, kind="ExternalInput").ap() for name, value in arrays.items()]
    out = nc.dram_tensor("outT", (C, T * B), F32, kind="ExternalOutput").ap()
    build(nc, *aps, out)
    result = run_bass_kernel_spmd(nc, [arrays], core_ids=[0])
    return np.asarray(result.results[0]["outT"]).reshape(C, T, B).transpose(2, 1, 0)
```

```python
from contextlib import ExitStack

import numpy as np
import concourse.bass as bass
from concourse import mybir

F32 = mybir.dt.float32
BF16 = mybir.dt.bfloat16
ALU = mybir.AluOpType
ACT = mybir.ActivationFunctionType
AX = mybir.AxisListType

B, T, C = 16, 512, 128
H, N = 16, 8
STEPS = 32
COLS = STEPS * B
CHUNKS = T // STEPS
QUARTER = 8
QCOLS = QUARTER * B
QUARTERS = STEPS // QUARTER
STATE = N * B
E, I = 4, 512
PICKS = 2 * 32 + E
J = I // C
RING = 2
MOE_STEPS = (19, 20, 21, 22, 22, 23, 24, 24, 25, 25, 26, 27, 28, 28, 29, 29)
LOOP_START = 4
DW = 64
DECAY = float(np.exp(-0.5))
CONSTS = 26

VECS = ["ln_pre_w", "ln_pre_b", "ln_attn_w", "ln_attn_b", "ln_ffn_w", "ln_ffn_b",
        "x_r", "x_w", "x_k", "x_v", "x_a", "x_g", "w0", "a0", "k_k", "k_a", "r_k",
        "gn_w", "gn_b", "ffn_x_k"]
FFN_VECS = ["bo", "ln_gamma", "ln_beta"]
V = {name: n for n, name in enumerate(VECS + FFN_VECS)}
NV = len(V)

M = {}
_at = 0
for _name, _w in [("W_k", C), ("w1", DW), ("a1", DW), ("W_v", C), ("W_r", C), ("g1", C), ("g2", C), ("W_o", C), ("w2_a2", C),
                  ("ffn1", J * C), ("ffn2", J * C), ("router", E), ("W1", E * I), ("Wo", J * C)]:
    M[_name] = _at
    _at += _w
NM = _at

K = {}
_at = 0
for _name, _w in [("center", C), ("mean", C), ("mean8", C), ("sum8", C), ("ident", C),
                  ("gather", N * C), ("rank", 4 * E)]:
    K[_name] = _at
    _at += _w
NK = _at


class Chunk:

    def __init__(self, base, off):
        self.base, self.off = base, off
        self.slot = off % RING

    def __add__(self, n):
        return Chunk(self.base, self.off + n)

    def has(self, back=0):
        return not isinstance(self.base, int) or 0 <= self.off - back < CHUNKS

    def count(self, done=1, per=1):
        if isinstance(self.base, int):
            return self.off * per + done
        return self.base * per + (self.off * per + done)

    def cols(self, eng):
        if isinstance(self.base, int):
            return slice(self.off * COLS, (self.off + 1) * COLS)
        return bass.ds(eng.snap(self.base * COLS + self.off * COLS), COLS)


def settled(eng, value):
    return value if isinstance(value, int) else eng.to_reg(value)


class Part:

    def __init__(self, pieces):
        self.pieces, self.at = pieces, -1

    def upto(self, step):
        while self.at <= step:
            self.at = next(self.pieces, 10 ** 6)


def build(nc, xT, mats, vecs, consts, b1_in, out):
    with ExitStack() as ctx:
        def sb(name, cols, dtype=F32, rows=128):
            return ctx.enter_context(nc.sbuf_tensor(name, [rows, cols], dtype))

        def ring(name, cols):
            return [sb(f"{name}{n}", cols) for n in range(RING)]

        def single(name, cols):
            return [sb(name, cols)] * RING

        def bank(name):
            return ctx.enter_context(nc.psum_tensor(name, [128, 512], F32))

        def sem(name):
            return ctx.enter_context(nc.semaphore(name))

        mat, vec, con = sb("mat", NM), sb("vec", NV), sb("con", NK)
        half_w0, half_a0, half_ka, rest_ka = (sb(n, 1) for n in ("half_w0", "half_a0", "half_ka", "rest_ka"))
        ident_bf = sb("ident_bf", C, BF16)
        b1_all = sb("b1_all", I, BF16)
        bo_c = sb("bo_c", 1)
        half_col, half_g2 = sb("half_col", 1), sb("half_g2", 1)
        scan_keep = sb("scan_keep", COLS)
        eps = {1e-5: sb("eps_ln", 1), 1e-5 ** 2: sb("eps_sq", 1), 6.4e-4: sb("eps_gn", 1), 1e-12: sb("eps_last", 1)}
        eps_ln, eps_sq, eps_gn, eps_last = (tile[:] for tile in eps.values())

        def w(name, n=0, width=C):
            return mat[:, M[name] + n * width:M[name] + (n + 1) * width]

        def k(name, n=0, width=C):
            return con[:, K[name] + n * width:K[name] + (n + 1) * width]

        def v(name):
            return vec[:, V[name]:V[name] + 1]

        x_in, x_res = single("x_in", COLS), single("x_res", COLS)
        x1, x1_keep, xn = ring("x1", COLS), sb("x1_keep", COLS), single("xn", B + COLS)
        a_t, b_t, k_t, r_t = ring("a_t", COLS), ring("b_t", COLS), ring("k_t", COLS), ring("r_t", COLS)
        p_all = ring("p_all", B + COLS)
        val, gate, bonus = sb("val", COLS), ring("gate", COLS), ring("bonus", COLS)
        val_rep = [sb(f"val_rep{n}", N // 2 * C) for n in range(2)]
        val_tm = ring("val_tm", COLS)
        xf, x2x = single("xf", B + COLS), single("x2x", COLS)

        sq_p, lv_p, rs_p, xh_p = (sb(n, COLS) for n in ("sq_p", "lv_p", "rs_p", "xh_p"))
        dx = sb("dx", COLS)
        mix = {q: sb(f"mix_{q}", COLS) for q in "wkag"}
        mix["v"], mix["r"] = mix["w"], mix["k"]
        key, k2, th_g, dec_bt, cum_bt = (sb(n, COLS) for n in ("key", "k2", "th_g", "dec_bt", "cum_bt"))
        low = sb("low", COLS)
        th_w, low_a = low[0:DW, :], low[DW:2 * DW, :]
        rkb, kk, kki, inv_p, th_a = mix["w"], mix["a"], mix["g"], dec_bt, dx
        rec = sb("rec", COLS)
        state = sb("state", (STEPS + 1) * STATE)
        s_a, upd, plus_kv = sb("s_a", STATE), sb("upd", STATE), sb("plus_kv", 2 * STATE)
        kv = sb("kv", 2 * QUARTER * STATE)
        s_r = sb("s_r", 2 * QUARTER * STATE)
        o_sb, sq_m, rs_m, y_m, z_m = (sb(n, COLS) for n in ("o_sb", "sq_m", "rs_m", "y_m", "z_m"))
        x2, kf = o_sb, z_m
        hid = [sb(f"hid{j}", COLS) for j in range(J)]
        y1, y1b, y2, sq_f, rs_f = (sb(n, COLS) for n in ("y1", "y1b", "y2", "sq_f", "rs_f"))
        h = ring("h", COLS)
        best, score, best2 = sb("best", 4), sb("score", 4 * E), sb("best2", 4)
        eq = sb("eq", 4 * E)
        onehot = sb("onehot", 4 * PICKS, BF16)
        pick = sb("pick", COLS, BF16)
        h_e = [sb(f"h_e{e}", COLS) for e in range(E)]
        act_j = [sb(f"act{j}", COLS) for j in range(J)]
        b1_rows, b1_rest, b1_part = hid[0], hid[1], hid[2][:].bitcast(BF16)[:, 0:I]
        wo_turned = act_j[0]
        res = single("res", COLS)

        sa_ps, o_ps, vb_ps = bank("sa_ps"), bank("o_ps"), bank("vb_ps")
        pre_a, pre_b, mid_ps, fin_a, fin_b = (bank(n) for n in ("pre_a", "pre_b", "mid_ps", "fin_a", "fin_b"))
        bf = lambda b: b[:].bitcast(BF16)

        names = """x_in x_res stored consts_in w_in consts_ready
            wo_turned wo_sb wo_c bo_c c0 sq0 j0 ln0 rs0 xh0 x1 x1_keep c1 sq1 j1 ln1 rs1 xh1 xn carry dx mix_w mix_a mix_k mix_v mix_r mix_g
            w1 th_w a1 low_a k key v val_tm val_rep vt val r rec g1 th_g w2 th_d a2 th_a dec cum p inv_p
            sqk kks nrm lnk rk kk kki b_t a_t ka_f k2 k_t r_t rkb rkb_ps bonus bonus_b g2 gate
            state s_a sa plus_kv upd vb kv s_r o
            o_sb gsq gj gln grs gxh gaff gg wo x2 x2x fc fsq fj fln frs fxh xf fcarry fdx kf
            f1 relu hid
            f2 y1 y1b ec esq ej eln ers h router best eq score best2 onehot masks h_e pick_ps pick moe act
            mo y2 lsq lj lvar lln lrs lxh res""".split()
        s = {n: sem("s_" + n) for n in names}
        block = ctx.enter_context(nc.Block())

        def bt(ap):
            return ap.rearrange("p (b t) -> p t b", b=B)

        def tb(ap, t=STEPS):
            return ap.rearrange("p (t b) -> p t b", t=t)

        def over_i(ap):
            return ap.unsqueeze(1).broadcast_to([128, N, B])

        def st(n):
            return state[:, n * STATE:(n + 1) * STATE]

        def pipeline(eng, fill, parts, scan_step, finish, before_step=lambda t: None):
            fill()

            def iteration(c):
                stages = [Part(make(c + skew)) for skew, make in parts
                          if (c + skew).has()]
                scanning = c.has()
                for t in range(STEPS):
                    before_step(t)
                    if scanning and scan_step:
                        scan_step(c, t, stages)
                    else:
                        for stage in stages:
                            stage.upto(t)
                for stage in stages:
                    stage.upto(10 ** 5)

            for c in (-1, 0, 1):
                if c < 0:
                    for n, wanted in ((0, 2), (0, 1), (1, 2)):
                        for skew, make in parts:
                            if skew == wanted:
                                Part(make(Chunk(0, n))).upto(10 ** 5)
                else:
                    iteration(Chunk(0, c))
            iteration(Chunk(0, 2))
            iteration(Chunk(0, 3))
            loops = (CHUNKS - 1 - LOOP_START) // RING
            with eng.Fori(LOOP_START, LOOP_START + RING * (loops - 1) + 1, RING) as first:
                for n in range(RING):
                    iteration(Chunk(first, n))
            for c in range(LOOP_START + RING * loops, CHUNKS + 3):
                iteration(Chunk(0, c))
            finish()

        last_pre = CHUNKS - 1

        @block.sync
        def _(sp):
            def fill():
                sp.dma_start(con[:], consts).then_inc(s["consts_in"], 16)
                sp.dma_start(vec[:], vecs).then_inc(s["consts_in"], 16)
                sp.dma_start(mat[:], mats).then_inc(s["w_in"], 16)
                sp.wait_ge(s["consts_ready"], 1)
                for n in range(3):
                    sp.dma_start(b1_rows[32 * n:32 * n + E, :], b1_in).then_inc(s["w_in"], 16)

            def norm(c):
                cols, last = c.cols(sp), settled(sp, (c + -1).count()) if c.has(1) else None
                sp.wait_ge(s["consts_in"], 32)
                if c.has(1):
                    sp.wait_ge(s["c0"], last)
                sp.dma_start(x_in[c.slot][:], xT[:, cols]).then_inc(s["x_in"], 16)
                yield 1

            def mid(c):
                cols, last = c.cols(sp), settled(sp, (c + -1).count()) if c.has(1) else None
                sp.wait_ge(s["w_in"], 64)
                if c.has(1):
                    sp.wait_ge(s["x2x"], last)
                sp.dma_start(x_res[c.slot][:], xT[:, cols]).then_inc(s["x_res"], 16)
                yield 1

            def last_norm(c):
                yield 24
                cols, now = c.cols(sp), settled(sp, c.count())
                sp.wait_ge(s["w_in"], 64)
                sp.wait_ge(s["res"], now)
                sp.dma_start(out[:, cols], res[c.slot][:]).then_inc(s["stored"], 16)
                yield 25

            def finish():
                sp.wait_ge(s["stored"], 16 * CHUNKS)

            pipeline(nc.sync, fill, [(2, norm), (-1, mid), (-3, last_norm)], None, finish)

        @block.tensor
        def _(pe):
            mm = nc.tensor.matmul

            def one(bank_, lhsT, rhs, name):
                return mm(bank_, lhsT, rhs, start=True, stop=True).then_inc(s[name], 1)

            def fill():
                pe.wait_ge(s["consts_in"], 32)
                pe.wait_ge(s["w_in"], 64)
                pe.wait_ge(s["consts_ready"], CONSTS)
                for j in range(J):
                    last = nc.tensor.transpose(fin_a[:, j * C:(j + 1) * C], w("Wo", j), k("ident"))
                last.then_inc(s["wo_turned"], 1)
                mm(fin_b[:, 0:1], k("center"), v("bo"), start=True, stop=True, skip_group_check=True)
                mm(fin_b[:, 1:2], w("g2"), half_col[:], start=False, stop=True,
                   skip_group_check=True).then_inc(s["bo_c"], 1)
                pe.wait_ge(s["wo_sb"], 1)
                for j in range(J):
                    last = mm(fin_a[:, j * C:(j + 1) * C], wo_turned[:, j * C:(j + 1) * C], k("center"),
                              start=(j == 0), stop=True, skip_group_check=True)
                last.then_inc(s["wo_c"], 1)
                pe.wait_ge(s["wo_sb"], 4)

            def spread(c, q, half):
                pe.wait_ge(s["val_rep"], c.count(2 * q + half + 1, 2 * QUARTERS))
                before = c.count(2 * q + half, 2 * QUARTERS)
                if not (isinstance(before, int) and before == 0):
                    pe.wait_ge(s["kv"], before)
                for n in range(N // 2):
                    last = nc.tensor.transpose(vb_ps[:, n * QCOLS:(n + 1) * QCOLS],
                                               val_rep[half][:, n * C:(n + 1) * C], k("ident"))
                last.then_inc(s["vb"], 1)

            def outputs(c, q, half):
                if half == 0:
                    pe.wait_ge(s["s_r"], c.count(4 * q + 4, 4 * QUARTERS))
                    if q == 0 and c.has(1):
                        pe.wait_ge(s["o_sb"], (c + -1).count())
                part = s_r[:, (q % 2) * QUARTER * STATE:(q % 2 + 1) * QUARTER * STATE]
                part = part.rearrange("p (t i b) -> p i t b", t=QUARTER, i=N)
                for n in range(N // 2):
                    i = half * N // 2 + n
                    last = mm(o_ps[:, q * QCOLS:(q + 1) * QCOLS], k("gather", i), part[:, i],
                              start=(i == 0), stop=(i == N - 1), skip_group_check=True)
                if half:
                    last.then_inc(s["o"], 1)

            def scan_step(c, t, stages):
                pe.wait_ge(s["s_a"], c.count(t + 1, STEPS))
                mm(sa_ps[:, 0:STATE], k("sum8"), s_a[:], start=True, stop=True).then_inc(s["sa"], 1)
                q, at = divmod(t, QUARTER)
                nxt = (c, q + 1) if q + 1 < QUARTERS else (c + 1, 0)
                if at in (1, 2) and nxt[0].has():
                    if t == QUARTER + 1 and c.has(1):
                        pe.wait_ge(s["gln"], (c + -1).count())
                    if t == 2 * QUARTER + 1 and c.has(3):
                        pe.wait_ge(s["lvar"], (c + -3).count())
                    if t == 3 * QUARTER + 1 and c.has(1):
                        pe.wait_ge(s["fln"], (c + -1).count())
                    spread(*nxt, at - 1)
                done = (c, q - 1) if q else (c + -1, QUARTERS - 1)
                if at in (3, 4) and done[0].has():
                    outputs(*done, at - 3)
                for stage in stages:
                    stage.upto(t)

            def norm(c):
                yield 30
                pe.wait_ge(s["x_in"], c.count(16, 16))
                if c.has(1):
                    pe.wait_ge(s["bonus"], (c + -1).count())
                one(pre_a[:], k("center"), x_in[c.slot][:], "c0")

            def pre(c):
                pe.wait_ge(s["sq0"], c.count())
                if c.has(1):
                    pe.wait_ge(s["gate"], (c + -1).count())
                one(pre_b[:], k("mean"), sq_p[:], "j0")
                yield 5
                pe.wait_ge(s["x1"], c.count())
                one(pre_a[:], k("center"), x1[c.slot][:], "c1")
                yield 7
                pe.wait_ge(s["sq1"], c.count())
                pe.wait_ge(s["ln0"], c.count())
                one(pre_b[:], k("mean"), sq_p[:], "j1")
                yield 13
                pe.wait_ge(s["mix_w"], c.count())
                pe.wait_ge(s["mix_a"], c.count())
                pe.wait_ge(s["xh1"], c.count())
                mm(pre_a[0:DW, :], w("w1", 0, DW), mix["w"][:], start=True, stop=True).then_inc(s["w1"], 1)
                mm(pre_a[DW:2 * DW, :], w("a1", 0, DW), mix["a"][:], start=True, stop=True).then_inc(s["a1"], 1)
                yield 14
                pe.wait_ge(s["mix_k"], c.count())
                pe.wait_ge(s["ln1"], c.count())
                one(pre_b[:], w("W_k"), mix["k"][:], "k")
                yield 15
                pe.wait_ge(s["th_w"], c.count())
                pe.wait_ge(s["low_a"], c.count())
                pe.wait_ge(s["key"], c.count())
                one(pre_a[:], w("w2_a2")[0:DW, :], th_w, "w2")
                one(pre_b[:], w("w2_a2")[DW:2 * DW, :], low_a, "a2")
                yield 16
                pe.wait_ge(s["mix_v"], c.count())
                pe.wait_ge(s["th_d"], c.count())
                for n in range(QUARTERS):
                    last = mm(pre_a[:, n * C:(n + 1) * C], mix["v"][:, n * QCOLS:(n + 1) * QCOLS], w("W_v"),
                              start=(n == 0), stop=True, skip_group_check=True)
                last.then_inc(s["v"], 1)
                pe.wait_ge(s["mix_g"], c.count())
                pe.wait_ge(s["th_a"], c.count())
                one(pre_b[:], w("g1"), mix["g"][:], "g1")
                yield 17
                pe.wait_ge(s["val_tm"], c.count())
                for n in range(QUARTERS):
                    last = nc.tensor.transpose(pre_a[:, n * QCOLS:(n + 1) * QCOLS],
                                               val_tm[c.slot][:, n * C:(n + 1) * C], k("ident"))
                last.then_inc(s["vt"], 1)
                yield 18
                pe.wait_ge(s["sqk"], c.count())
                pe.wait_ge(s["th_g"], c.count())
                one(pre_b[:], k("sum8"), sq_p[:], "kks")
                pe.wait_ge(s["mix_r"], c.count())
                pe.wait_ge(s["val"], c.count())
                one(pre_a[:], w("W_r"), mix["r"][:], "r")
                yield 22
                pe.wait_ge(s["th_g"], c.count())
                pe.wait_ge(s["nrm"], c.count())
                one(pre_b[:], w("g2"), th_g[:], "g2")
                yield 23
                pe.wait_ge(s["rkb"], c.count())
                pe.wait_ge(s["rec"], c.count())
                one(pre_a[:], k("sum8"), rkb[:], "rkb_ps")
                yield 24

            def mid(c):
                if isinstance(c.base, int) and c.off == CHUNKS - 1:
                    outputs(c, QUARTERS - 1, 0)
                    outputs(c, QUARTERS - 1, 1)
                yield 6
                pe.wait_ge(s["gsq"], c.count())
                pe.wait_ge(s["kv"], vb_free(c + 1, 1))
                if c.has(1):
                    pe.wait_ge(s["fln"], (c + -1).count())
                one(vb_ps[:], k("mean8"), sq_m[:], "gj")
                yield 14
                pe.wait_ge(s["gg"], c.count())
                if c.has(1):
                    pe.wait_ge(s["y1"], (c + -1).count())
                if c.has(2):
                    pe.wait_ge(s["y2"], (c + -2).count())
                one(mid_ps[:], w("W_o"), z_m[:], "wo")
                yield 17
                pe.wait_ge(s["x2"], c.count())
                one(mid_ps[:], k("center"), x2[:], "fc")
                yield 21
                pe.wait_ge(s["fsq"], c.count())
                pe.wait_ge(s["gln"], c.count())
                pe.wait_ge(s["kv"], vb_free(c + 1, 3))
                if c.has(2):
                    pe.wait_ge(s["lvar"], (c + -2).count())
                one(vb_ps[:], k("mean"), sq_m[:], "fj")
                yield 22

            def vb_free(scan, quarter):
                n = scan.count(2 * quarter + 2, 2 * QUARTERS)
                return min(n, CHUNKS * 2 * QUARTERS) if isinstance(n, int) else n

            def fin(c):
                for j in range(J):
                    yield j
                    pe.wait_ge(s["kf"], c.count())
                    if j == 1 and c.has(1):
                        pe.wait_ge(s["act"], c.count(0, J))
                    if j >= 2:
                        pe.wait_ge(s["relu"], c.count(j - 1, J))
                    one((mid_ps, fin_a)[j % 2][:], w("ffn1", j), kf[:], "f1")
                for j in range(J):
                    yield 4 + j
                    pe.wait_ge(s["hid"], c.count(max(j + 1, 3), J))
                    last = mm(mid_ps[:], w("ffn2", j), hid[j][:], start=(j == 0), stop=(j == J - 1))
                last.then_inc(s["f2"], 1)
                yield 9
                pe.wait_ge(s["y1"], c.count())
                one(fin_a[:], k("center"), y1[:], "ec")
                yield 10
                pe.wait_ge(s["esq"], c.count())
                if c.has(1):
                    pe.wait_ge(s["act"], c.count(0, J))
                one(fin_b[:], k("mean"), sq_f[:], "ej")
                yield 13
                pe.wait_ge(s["h"], c.count())
                for n in range(4):
                    last = mm(fin_a[:, n * E:(n + 1) * E], h[c.slot][:, n * C:(n + 1) * C], w("router", 0, E),
                              start=(n == 0), stop=True, skip_group_check=True)
                last.then_inc(s["router"], 1)
                yield 16
                pe.wait_ge(s["onehot"], c.count(3, 3))
                pe.wait_ge(s["eln"], c.count())
                for e in range(E):
                    to = bf(fin_b if e < 2 else fin_a)
                    for n in range(4):
                        last = nc.tensor.transpose(
                            to[:, (e % 2) * COLS + n * C:(e % 2) * COLS + (n + 1) * C],
                            onehot[:, n * PICKS + e:n * PICKS + e + 1].broadcast_to([128, C]), ident_bf[:])
                    if e % 2:
                        last.then_inc(s["masks"], 1)
                yield 18
                pe.wait_ge(s["h_e"], c.count(2, E))
                for n in range(4):
                    last = nc.tensor.transpose(bf(fin_b)[0:PICKS, n * C:(n + 1) * C],
                                               onehot[:, n * PICKS:(n + 1) * PICKS], ident_bf[:])
                last.then_inc(s["pick_ps"], 1)
                steps = iter(MOE_STEPS)
                for j in range(J):
                    for e in range(E):
                        yield next(steps)
                        if j == 0:
                            pe.wait_ge(s["h_e"], c.count(e + 1, E))
                        if j == 0 and e == 0:
                            pe.wait_ge(s["pick"], c.count())
                        if j == 1 and e == 0:
                            pe.wait_ge(s["h_e"], c.count(4, E))
                        if j >= 2 and e == 0:
                            pe.wait_ge(s["act"], c.count(j - 1, J))
                        mm((fin_b, fin_a)[j % 2][:], mat[:, M["W1"] + e * I + j * C:M["W1"] + e * I + (j + 1) * C],
                           h_e[e][:], start=(e == 0), stop=False)
                    mm((fin_b, fin_a)[j % 2][:], b1_all[0:PICKS, j * C:(j + 1) * C], pick[0:PICKS, :],
                       start=False, stop=True).then_inc(s["moe"], 1)

            def last_norm(c):
                if (c + 1).has():
                    yield 9
                    pe.wait_ge(s["y1"], (c + 1).count())
                for j in range(J):
                    yield 9 + j
                    pe.wait_ge(s["act"], c.count(j + 1, J))
                    last = mm(mid_ps[:], w("Wo", j), act_j[j][:], start=(j == 0), stop=(j == J - 1))
                last.then_inc(s["mo"], 1)
                yield 15
                pe.wait_ge(s["lsq"], c.count())
                pe.wait_ge(s["kv"], vb_free(c + 3, 2))
                pe.wait_ge(s["gln"], newest_mid(c))
                one(vb_ps[:], k("mean"), sq_f[:], "lj")
                yield 16

            def newest_mid(c):
                n = (c + 2).count()
                return min(n, CHUNKS) if isinstance(n, int) else n

            def first_quarter(c):
                yield from pre(c)
                if isinstance(c.base, int) and c.off == 0:
                    spread(c, 0, 0)
                    spread(c, 0, 1)

            pipeline(nc.tensor, fill, [(2, norm), (1, first_quarter), (-1, mid), (-2, fin), (-3, last_norm)], scan_step,
                     lambda: None)

        @block.scalar
        def _(act):
            f = nc.scalar.activation

            def fill():
                act.wait_ge(s["consts_in"], 32)
                act.wait_ge(s["consts_ready"], CONSTS)
                nc.scalar.preload_act_table_set("natural_log_exp_and_others")

            def replicate(c, q, half):
                act.wait_ge(s["val_tm"], c.count())
                before = c.count(2 * q + half - 1, 2 * QUARTERS)
                if not isinstance(before, int) or before > 0:
                    act.wait_ge(s["vb"], before)
                heads = val_tm[c.slot][:, q * C:(q + 1) * C].rearrange("p (h i) -> p i h", i=N)
                heads = heads[:, half * N // 2:(half + 1) * N // 2].unsqueeze(3).broadcast_to([128, N // 2, H, N])
                to = val_rep[half][:].rearrange("p (i h j) -> p i h j", i=N // 2, h=H)
                f(to, heads, ACT.Identity).then_inc(s["val_rep"], 1)

            def scan_step(c, t, stages):
                q, at = divmod(t, QUARTER)
                nxt = (c, q + 1) if q + 1 < QUARTERS else (c + 1, 0)
                if at in (0, 1) and nxt[0].has():
                    replicate(*nxt, at)
                for stage in stages:
                    stage.upto(t)

            def rsqrt(c, var, eps, lv, rs, n_in, n_ln, n_rs, scale=1.0):
                act.wait_ge(s[n_in], c.count())
                f(lv, var, ACT.Ln, bias=eps, scale=scale).then_inc(s[n_ln], 1)
                act.wait_ge(s[n_ln], c.count())
                f(rs, lv, ACT.Exp, scale=-0.5).then_inc(s[n_rs], 1)

            def norm(c):
                yield 30
                act.wait_ge(s["c0"], c.count())
                if c.has(1):
                    act.wait_ge(s["kks"], (c + -1).count())
                f(sq_p[:], pre_a[:], ACT.Square).then_inc(s["sq0"], 1)

            def pre(c):
                yield 1
                if c.has(1):
                    act.wait_ge(s["kk"], (c + -1).count())
                rsqrt(c, pre_b[:], eps_sq, lv_p[:], rs_p[:], "j0", "ln0", "rs0", scale=1.0 + 1e-5)
                yield 3
                act.wait_ge(s["xh0"], c.count())
                if c.has(2):
                    act.wait_ge(s["x1_keep"], (c + -2).count())
                f(x1[c.slot][:], xh_p[:], ACT.Identity, bias=v("ln_pre_b"), scale=v("ln_pre_w")).then_inc(s["x1"], 1)
                yield 5
                act.wait_ge(s["c1"], c.count())
                act.wait_ge(s["j0"], c.count())
                f(sq_p[:], pre_a[:], ACT.Square).then_inc(s["sq1"], 1)
                if c.has(1):
                    act.wait_ge(s["xn"], (c + -1).count())
                    act.wait_ge(s["mix_r"], (c + -1).count())
                    f(xn[c.slot][:, 0:B], xn[c.slot][:, COLS:COLS + B], ACT.Identity).then_inc(s["carry"], 1)
                else:
                    f(xn[0][:, 0:B], scan_keep[:, 0:B], ACT.Identity, scale=0.0).then_inc(s["carry"], 1)
                yield 7
                act.wait_ge(s["xh0"], c.count())
                rsqrt(c, pre_b[:], eps_ln, lv_p[:], rs_p[:], "j1", "ln1", "rs1")
                yield 9
                act.wait_ge(s["xh1"], c.count())
                act.wait_ge(s["carry"], c.count())
                f(xn[c.slot][:, B:B + COLS], xh_p[:], ACT.Identity, bias=v("ln_attn_b"),
                  scale=v("ln_attn_w")).then_inc(s["xn"], 1)
                yield 13
                act.wait_ge(s["w1"], c.count())
                act.wait_ge(s["a1"], c.count())
                if c.has(1):
                    act.wait_ge(s["w2"], (c + -1).count())
                    act.wait_ge(s["a2"], (c + -1).count())
                f(th_w, pre_a[0:DW, :], ACT.Tanh).then_inc(s["th_w"], 1)
                f(low_a, pre_a[DW:2 * DW, :], ACT.Identity).then_inc(s["low_a"], 1)
                yield 14
                act.wait_ge(s["k"], c.count())
                if c.has(1):
                    act.wait_ge(s["k2"], (c + -1).count())
                    act.wait_ge(s["kk"], (c + -1).count())
                f(key[:], pre_b[:], ACT.Identity).then_inc(s["key"], 1)
                act.wait_ge(s["key"], c.count())
                act.wait_ge(s["j1"], c.count())
                f(sq_p[:], key[:], ACT.Square, scale=v("k_k")).then_inc(s["sqk"], 1)
                yield 15
                act.wait_ge(s["w2"], c.count())
                if c.has(1):
                    act.wait_ge(s["k_t"], (c + -1).count())
                    act.wait_ge(s["kki"], (c + -1).count())
                f(bt(dec_bt[:]), tb(pre_a[:]), ACT.Tanh, bias=half_w0[:], scale=0.5).then_inc(s["th_d"], 1)
                act.wait_ge(s["a2"], c.count())
                act.wait_ge(s["mix_r"], c.count())
                f(th_a[:], pre_b[:], ACT.Tanh, bias=half_a0[:], scale=0.5).then_inc(s["th_a"], 1)
                act.wait_ge(s["th_a"], c.count())
                if c.has(1):
                    act.wait_ge(s["k_t"], (c + -1).count())
                    act.wait_ge(s["rkb"], (c + -1).count())
                f(k2[:], th_a[:], ACT.Identity, bias=rest_ka[:], scale=half_ka[:]).then_inc(s["ka_f"], 1)
                yield 16
                act.wait_ge(s["v"], c.count())
                f(val_tm[c.slot][:], pre_a[:], ACT.Identity).then_inc(s["val_tm"], 1)
                act.wait_ge(s["g1"], c.count())
                if c.has(1):
                    act.wait_ge(s["g2"], (c + -1).count())
                f(th_g[:], pre_b[:], ACT.Tanh, scale=0.5).then_inc(s["th_g"], 1)
                yield 17
                act.wait_ge(s["vt"], c.count())
                if c.has(1):
                    act.wait_ge(s["bonus"], (c + -1).count())
                f(val[:], pre_a[:], ACT.Identity).then_inc(s["val"], 1)
                yield 18
                act.wait_ge(s["r"], c.count())
                if c.has(1):
                    act.wait_ge(s["r_t"], (c + -1).count())
                    act.wait_ge(s["rkb"], (c + -1).count())
                f(rec[:], pre_a[:], ACT.Identity).then_inc(s["rec"], 1)
                yield 20
                act.wait_ge(s["cum"], c.count())
                f(tb(p_all[c.slot][:, B:B + COLS]), bt(cum_bt[:]), ACT.Exp, scale=-DECAY).then_inc(s["p"], 1)
                f(tb(inv_p[:]), bt(cum_bt[:]), ACT.Exp, scale=DECAY).then_inc(s["inv_p"], 1)
                yield 21
                act.wait_ge(s["xh1"], c.count())
                rsqrt(c, lv_p[:], 0.0, lv_p[:], rs_p[:], "nrm", "lnk", "rk")
                yield 22
                act.wait_ge(s["g2"], c.count())
                f(gate[c.slot][:], pre_b[:], ACT.Identity, bias=half_g2[:], scale=0.5).then_inc(s["gate"], 1)
                yield 23

            def keep(c):
                yield 17
                act.wait_ge(s["x1"], c.count())
                if c.has(1):
                    act.wait_ge(s["x2"], (c + -1).count())
                f(x1_keep[:], x1[c.slot][:], ACT.Identity).then_inc(s["x1_keep"], 1)

            def mid(c):
                yield 5
                act.wait_ge(s["o"], c.count(QUARTERS, QUARTERS))
                if c.has(1):
                    act.wait_ge(s["fj"], (c + -1).count())
                f(sq_m[:], o_ps[:], ACT.Square).then_inc(s["gsq"], 1)
                if c.has(1):
                    act.wait_ge(s["fc"], (c + -1).count())
                    act.wait_ge(s["x2x"], (c + -1).count())
                f(o_sb[:], o_ps[:], ACT.Identity).then_inc(s["o_sb"], 1)
                yield 6
                if c.has(1):
                    act.wait_ge(s["fxh"], (c + -1).count())
                rsqrt(c, vb_ps[:], eps_gn, rs_m[:], rs_m[:], "gj", "gln", "grs")
                yield 18
                act.wait_ge(s["fc"], c.count())
                act.wait_ge(s["gj"], c.count())
                f(sq_m[:], mid_ps[:], ACT.Square).then_inc(s["fsq"], 1)
                if c.has(1):
                    act.wait_ge(s["xf"], (c + -1).count())
                    act.wait_ge(s["kf"], (c + -1).count())
                    f(xf[c.slot][:, 0:B], xf[c.slot][:, COLS:COLS + B], ACT.Identity).then_inc(s["fcarry"], 1)
                yield 21
                act.wait_ge(s["gxh"], c.count())
                rsqrt(c, vb_ps[:], eps_ln, rs_m[:], rs_m[:], "fj", "fln", "frs")
                yield 23
                act.wait_ge(s["fcarry"], c.count())
                act.wait_ge(s["fxh"], c.count())
                f(xf[c.slot][:, B:B + COLS], y_m[:], ACT.Identity, bias=v("ln_ffn_b"),
                  scale=v("ln_ffn_w")).then_inc(s["xf"], 1)

            def fin(c):
                for j in range(J):
                    yield j
                    act.wait_ge(s["f1"], c.count(j + 1, J))
                    if j == 0 and c.has(1):
                        act.wait_ge(s["f2"], (c + -1).count())
                    f(hid[j][:], (mid_ps, fin_a)[j % 2][:], ACT.Relu).then_inc(s["relu"], 1)
                    act.wait_ge(s["relu"], c.count(j + 1, J))
                    f(hid[j][:], hid[j][:], ACT.Square).then_inc(s["hid"], 1)
                yield 9
                act.wait_ge(s["ec"], c.count())
                if c.has(2):
                    act.wait_ge(s["lj"], (c + -2).count())
                f(sq_f[:], fin_a[:], ACT.Square).then_inc(s["esq"], 1)
                yield 10
                if c.has(2):
                    act.wait_ge(s["lxh"], (c + -2).count())
                rsqrt(c, fin_b[:], eps_ln, rs_f[:], rs_f[:], "ej", "eln", "ers")
                yield 18
                act.wait_ge(s["pick_ps"], c.count())
                if c.has(1):
                    act.wait_ge(s["moe"], c.count(0, J))
                f(pick[0:PICKS, :], bf(fin_b)[0:PICKS, 0:COLS], ACT.Identity).then_inc(s["pick"], 1)
                for j in range(J):
                    yield (23, 25, 28, 31)[j]
                    act.wait_ge(s["moe"], c.count(j + 1, J))
                    if j == 0 and c.has(1):
                        act.wait_ge(s["mo"], (c + -1).count())
                    f(act_j[j][:], (fin_b, fin_a)[j % 2][:], ACT.Gelu).then_inc(s["act"], 1)

            def last_norm(c):
                ahead = (c + 1) if (c + 1).has() else c
                yield 14
                act.wait_ge(s["y2"], c.count())
                act.wait_ge(s["ej"], ahead.count())
                f(sq_f[:], y2[:], ACT.Square).then_inc(s["lsq"], 1)
                yield 15
                act.wait_ge(s["lj"], c.count())
                act.wait_ge(s["h"], ahead.count())
                f(rs_f[:], vb_ps[:], ACT.Identity).then_inc(s["lvar"], 1)
                yield 19
                rsqrt(c, rs_f[:], eps_last, rs_f[:], rs_f[:], "lvar", "lln", "lrs")
                yield 20

            def tables(t):
                if t in (0, 19):
                    nc.scalar.preload_act_table_set("natural_log_exp_and_others")
                if t in (13, 23):
                    nc.scalar.preload_act_table_set("gelu_and_others")

            def first_quarter(c):
                yield from pre(c)
                if isinstance(c.base, int) and c.off == 0:
                    replicate(c, 0, 0)
                    replicate(c, 0, 1)

            pipeline(nc.scalar, fill, [(2, norm), (1, first_quarter), (0, keep), (-1, mid), (-2, fin), (-3, last_norm)],
                     scan_step, lambda: None, tables)

        @block.vector
        def _(dve):
            tt, ts, stt = nc.vector.tensor_tensor, nc.vector.tensor_scalar, nc.vector.scalar_tensor_tensor
            made = [0]

            def const(op):
                op.then_inc(s["consts_ready"], 1)
                made[0] += 1
                dve.wait_ge(s["consts_ready"], made[0])

            def fill():
                const(nc.vector.memset(b1_rows[:], 0.0))
                dve.wait_ge(s["consts_in"], 32)
                const(nc.vector.tensor_copy(ident_bf[:], k("ident")))
                const(ts(half_w0[:], v("w0"), 0.5, None, ALU.mult))
                const(ts(half_a0[:], v("a0"), 0.5, None, ALU.mult))
                const(ts(half_ka[:], v("k_a"), 0.5, None, ALU.mult))
                const(ts(rest_ka[:], half_ka[:], -1.0, 1.0, ALU.mult, ALU.add))
                const(nc.vector.memset(half_col[:], 0.5))
                const(nc.vector.memset(scan_keep[:], 1.0))
                const(nc.vector.memset(bt(scan_keep[:])[:, 0, :], 0.0))
                for value, tile in eps.items():
                    const(nc.vector.memset(tile[:], value))
                for n in range(RING):
                    const(nc.vector.memset(p_all[n][:, 0:B], 1.0))
                const(nc.vector.memset(onehot[:], 0.0))
                const(nc.vector.memset(b1_all[:], 0.0))
                dve.wait_ge(s["w_in"], 64)
                const(nc.vector.tensor_copy(b1_all[0:E, :], b1_rows[0:E, :]))
                for n in (1, 2):
                    const(nc.vector.tensor_copy(b1_part, b1_rows[:]))
                    const(tt(b1_rest[:], b1_rows[:], b1_part, ALU.subtract))
                    const(nc.vector.tensor_copy(b1_rows[:], b1_rest[:]))
                    const(nc.vector.tensor_copy(b1_all[32 * n:32 * n + E, :], b1_rows[32 * n:32 * n + E, :]))
                dve.wait_ge(s["wo_turned"], 1)
                nc.vector.tensor_copy(wo_turned[:], fin_a[:]).then_inc(s["wo_sb"], 1)
                dve.wait_ge(s["bo_c"], 1)
                nc.vector.tensor_copy(bo_c[:], fin_b[:, 0:1]).then_inc(s["wo_sb"], 1)
                nc.vector.tensor_copy(half_g2[:], fin_b[:, 1:2]).then_inc(s["wo_sb"], 1)
                dve.wait_ge(s["wo_c"], 1)
                nc.vector.tensor_copy(w("Wo", 0, J * C), fin_a[:]).then_inc(s["wo_sb"], 1)
                nc.vector.memset(st(0), 0.0).then_inc(s["state"], 1)

            def ib(ap):
                return ap.rearrange("p (i b) -> p i b", i=N)

            def spread_kv(c, q, half):
                if half == 0:
                    dve.wait_ge(s["k_t"], c.count())
                dve.wait_ge(s["vb"], c.count(2 * q + half + 1, 2 * QUARTERS))
                part = kv[:, (q % 2) * QUARTER * STATE:(q % 2 + 1) * QUARTER * STATE]
                part = part.rearrange("p (t i b) -> p i t b", t=QUARTER, i=N)[:, half * 4:half * 4 + 4]
                keys = k_t[c.slot][:, q * QCOLS:(q + 1) * QCOLS].rearrange("p (t b) -> p t b", t=QUARTER)
                tt(part, vb_ps[:].rearrange("p (i t b) -> p i t b", i=N // 2, t=QUARTER),
                   keys.unsqueeze(1).broadcast_to([128, N // 2, QUARTER, B]), ALU.mult).then_inc(s["kv"], 1)

            def scan_step(c, t, stages):
                if t == 0 and c.has(1):
                    dve.wait_ge(s["state"], c.count(0, STEPS + 1))
                    last = p_all[(c + -1).slot][:, COLS:COLS + B]
                    tt(ib(st(0)), ib(st(STEPS)), over_i(last), ALU.mult).then_inc(s["state"], 1)
                if t == 0:
                    dve.wait_ge(s["a_t"], c.count())
                dve.wait_ge(s["state"], c.count(t + 1, STEPS + 1))
                tt(ib(s_a[:]), ib(st(t)), over_i(a_t[c.slot][:, t * B:(t + 1) * B]), ALU.mult).then_inc(s["s_a"], 1)
                q, at = divmod(t, QUARTER)
                nxt = (c, q + 1) if q + 1 < QUARTERS else (c + 1, 0)
                if at in (2, 3) and nxt[0].has():
                    spread_kv(*nxt, at - 2)
                for stage in stages:
                    stage.upto(t)
                if t == 0:
                    dve.wait_ge(s["b_t"], c.count())
                dve.wait_ge(s["sa"], c.count(t + 1, STEPS))
                tt(ib(upd[:]), ib(sa_ps[:, 0:STATE]), over_i(b_t[c.slot][:, t * B:(t + 1) * B]),
                   ALU.mult).then_inc(s["upd"], 1)
                dve.wait_ge(s["upd"], c.count(t + 1, STEPS))
                dve.wait_ge(s["plus_kv"], c.count(t + 1, STEPS))
                tt(st(t + 1), upd[:], plus_kv[:, (t % 2) * STATE:(t % 2 + 1) * STATE], ALU.add).then_inc(s["state"], 1)

            def pre(c):
                yield 3
                dve.wait_ge(s["rs0"], c.count())
                if c.has(1):
                    dve.wait_ge(s["xn"], (c + -1).count())
                tt(xh_p[:], pre_a[:], rs_p[:], ALU.mult).then_inc(s["xh0"], 1)
                yield 9
                dve.wait_ge(s["rs1"], c.count())
                dve.wait_ge(s["x1"], c.count())
                tt(xh_p[:], pre_a[:], rs_p[:], ALU.mult).then_inc(s["xh1"], 1)
                yield 10
                dve.wait_ge(s["xn"], c.count())
                if c.has(1):
                    dve.wait_ge(s["b_t"], (c + -1).count())
                    dve.wait_ge(s["ka_f"], (c + -1).count())
                tt(dx[:], xn[c.slot][:, 0:COLS], xn[c.slot][:, B:B + COLS], ALU.subtract).then_inc(s["dx"], 1)
                now = xn[c.slot][:, B:B + COLS]
                for q, read, at in (("w", "rkb_ps", 11), ("a", "a_t", 12), ("k", "r", 13), ("v", "w1", 14),
                                    ("g", "b_t", 15), ("r", "k", 16)):
                    yield at
                    if q == "w":
                        dve.wait_ge(s["dx"], c.count())
                    if q in "vr":
                        dve.wait_ge(s[read], c.count())
                    elif c.has(1):
                        dve.wait_ge(s[read], (c + -1).count())
                    stt(mix[q][:], dx[:], v("x_" + q), now, ALU.mult, ALU.add).then_inc(s["mix_" + q], 1)
                yield 18
                dve.wait_ge(s["th_d"], c.count())
                ts(dec_bt[:], dec_bt[:], 0.5, 0.5, ALU.mult, ALU.add).then_inc(s["dec"], 1)
                yield 19
                dve.wait_ge(s["dec"], c.count())
                if c.has(1):
                    dve.wait_ge(s["inv_p"], (c + -1).count())
                nc.vector.tensor_tensor_scan(cum_bt[:], scan_keep[:], dec_bt[:], 0.0,
                                             ALU.mult, ALU.add).then_inc(s["cum"], 1)
                yield 20
                dve.wait_ge(s["kks"], c.count())
                dve.wait_ge(s["rs1"], c.count())
                ts(lv_p[:], pre_b[:], 1e-24, None, ALU.max).then_inc(s["nrm"], 1)
                yield 21
                dve.wait_ge(s["rec"], c.count())
                dve.wait_ge(s["k2"], c.count())
                dve.wait_ge(s["v"], c.count())
                stt(rkb[:], rec[:], v("r_k"), k2[:], ALU.mult, ALU.mult).then_inc(s["rkb"], 1)
                yield 22
                dve.wait_ge(s["rk"], c.count())
                dve.wait_ge(s["key"], c.count())
                stt(kk[:], key[:], v("k_k"), rs_p[:], ALU.mult, ALU.mult).then_inc(s["kk"], 1)
                dve.wait_ge(s["inv_p"], c.count())
                tt(k_t[c.slot][:], k2[:], inv_p[:], ALU.mult).then_inc(s["k_t"], 1)
                yield 23
                dve.wait_ge(s["kk"], c.count())
                stt(kki[:], kk[:], 0.5, inv_p[:], ALU.mult, ALU.mult).then_inc(s["kki"], 1)
                yield 24
                dve.wait_ge(s["rkb_ps"], c.count())
                dve.wait_ge(s["val"], c.count())
                tt(bonus[c.slot][:], pre_a[:], val[:], ALU.mult).then_inc(s["bonus"], 1)
                yield 25
                dve.wait_ge(s["p"], c.count())
                stt(a_t[c.slot][:], kk[:], -1.0, p_all[c.slot][:, 0:COLS], ALU.mult, ALU.mult).then_inc(s["a_t"], 1)
                yield 26
                dve.wait_ge(s["kki"], c.count())
                dve.wait_ge(s["th_a"], c.count())
                stt(b_t[c.slot][:], th_a[:], 1.0, kki[:], ALU.add, ALU.mult).then_inc(s["b_t"], 1)
                yield 27

            def mid(c):
                yield 8
                dve.wait_ge(s["grs"], c.count())
                dve.wait_ge(s["o_sb"], c.count())
                tt(y_m[:], o_sb[:], rs_m[:], ALU.mult).then_inc(s["gxh"], 1)
                yield 9
                dve.wait_ge(s["gxh"], c.count())
                dve.wait_ge(s["bonus_b"], c.count())
                if c.has(1):
                    dve.wait_ge(s["f1"], c.count(0, J))
                stt(z_m[:], y_m[:], v("gn_w"), bonus[c.slot][:], ALU.mult, ALU.add).then_inc(s["gaff"], 1)
                yield 16
                dve.wait_ge(s["wo"], c.count())
                dve.wait_ge(s["x1_keep"], c.count())
                tt(x2[:], mid_ps[:], x1_keep[:], ALU.add).then_inc(s["x2"], 1)
                yield 23
                dve.wait_ge(s["frs"], c.count())
                tt(y_m[:], mid_ps[:], rs_m[:], ALU.mult).then_inc(s["fxh"], 1)
                yield 25
                dve.wait_ge(s["xf"], c.count())
                dve.wait_ge(s["fcarry"], c.count())
                now = xf[c.slot][:, B:B + COLS]
                tt(y_m[:], xf[c.slot][:, 0:COLS], now, ALU.subtract).then_inc(s["fdx"], 1)
                yield 27
                dve.wait_ge(s["fdx"], c.count())
                dve.wait_ge(s["wo"], c.count())
                stt(kf[:], y_m[:], v("ffn_x_k"), now, ALU.mult, ALU.add).then_inc(s["kf"], 1)

            def fin(c):
                yield 8
                dve.wait_ge(s["f2"], c.count())
                dve.wait_ge(s["x2x"], c.count())
                if c.has(1):
                    dve.wait_ge(s["ec"], (c + -1).count())
                    dve.wait_ge(s["y1b"], (c + -1).count())
                tt(y1[:], mid_ps[:], x2x[c.slot][:], ALU.add).then_inc(s["y1"], 1)
                yield 12
                dve.wait_ge(s["ers"], c.count())
                if c.has(2):
                    dve.wait_ge(s["y2"], (c + -2).count())
                tt(h[c.slot][:], fin_a[:], rs_f[:], ALU.mult).then_inc(s["h"], 1)
                yield 14
                dve.wait_ge(s["router"], c.count())
                logits = fin_a[:, 0:4 * E].rearrange("p (n e) -> p n e", e=E)
                rows = lambda a: a[:].rearrange("p (n e) -> p n e", e=E)
                every = lambda a: a[:].unsqueeze(2).broadcast_to([128, 4, E])
                nc.vector.tensor_reduce(best[:], logits, AX.X, ALU.max).then_inc(s["best"], 1)
                dve.wait_ge(s["best"], c.count())
                tt(rows(eq), logits, every(best), ALU.is_ge).then_inc(s["eq"], 1)
                dve.wait_ge(s["eq"], c.count())
                tt(score[:], eq[:], k("rank", 0, 4 * E), ALU.mult).then_inc(s["score"], 1)
                yield 15
                dve.wait_ge(s["score"], c.count())
                nc.vector.tensor_reduce(best2[:], rows(score), AX.X, ALU.max).then_inc(s["best2"], 1)
                dve.wait_ge(s["best2"], c.count())
                if c.has(1):
                    dve.wait_ge(s["pick_ps"], (c + -1).count())
                for n in range(3):
                    to = onehot[:].rearrange("p (n r) -> p n r", r=PICKS)[:, :, 32 * n:32 * n + E]
                    tt(to, rows(score), every(best2), ALU.is_equal).then_inc(s["onehot"], 1)
                for e in range(E):
                    yield (17, 17, 19, 20)[e]
                    dve.wait_ge(s["masks"], c.count(e // 2 + 1, 2))
                    if e == 0 and c.has(1):
                        dve.wait_ge(s["moe"], c.count(0, J))
                    mask = bf(fin_b if e < 2 else fin_a)[:, (e % 2) * COLS:(e % 2 + 1) * COLS]
                    tt(h_e[e][:], mask, h[c.slot][:], ALU.mult).then_inc(s["h_e"], 1)

            def last_norm(c):
                yield 13
                dve.wait_ge(s["mo"], c.count())
                if c.has(1):
                    dve.wait_ge(s["res"], (c + -1).count())
                stt(y2[:], mid_ps[:], bo_c[:], h[c.slot][:], ALU.add, ALU.add).then_inc(s["y2"], 1)
                yield 21
                dve.wait_ge(s["lrs"], c.count())
                tt(y2[:], y2[:], rs_f[:], ALU.mult).then_inc(s["lxh"], 1)
                yield 24
                dve.wait_ge(s["lxh"], c.count())
                dve.wait_ge(s["y1b"], c.count())
                if c.has(1):
                    dve.wait_ge(s["stored"], (c + -1).count(16, 16))
                stt(res[c.slot][:], y2[:], v("ln_gamma"), y1b[:], ALU.mult, ALU.add).then_inc(s["res"], 1)

            def first_quarter(c):
                yield from pre(c)
                if isinstance(c.base, int) and c.off == 0:
                    spread_kv(c, 0, 0)
                    spread_kv(c, 0, 1)

            pipeline(nc.vector, fill, [(1, first_quarter), (-1, mid), (-2, fin), (-3, last_norm)], scan_step,
                     lambda: None)

        @block.gpsimd
        def _(pool):
            tt, ts = nc.gpsimd.tensor_tensor, nc.gpsimd.tensor_scalar

            def fill():
                pool.wait_ge(s["consts_in"], 32)
                pool.wait_ge(s["consts_ready"], CONSTS)
                nc.gpsimd.memset(xf[0][:, 0:B], 0.0).then_inc(s["fcarry"], 1)

            def read_out(c, n):
                q, at = divmod(2 * n, QUARTER)
                if at == 0:
                    if n == 0:
                        pool.wait_ge(s["r_t"], c.count())
                    before = c.count(q - 1, QUARTERS)
                    if not isinstance(before, int) or before > 0:
                        pool.wait_ge(s["o"], before)
                first = (q % 2) * QUARTER * STATE + at * STATE
                part = s_r[:, first:first + 2 * STATE].rearrange("p (t i b) -> p t i b", t=2, i=N)
                states = state[:, (2 * n + 1) * STATE:(2 * n + 3) * STATE].rearrange("p (t i b) -> p t i b", t=2, i=N)
                r = r_t[c.slot][:, 2 * n * B:(2 * n + 2) * B].rearrange("p (t b) -> p t b", t=2)
                tt(part, states, r.unsqueeze(2).broadcast_to([128, 2, N, B]), ALU.mult).then_inc(s["s_r"], 1)

            def scan_step(c, t, stages):
                if t % QUARTER == 0:
                    pool.wait_ge(s["kv"], c.count(2 * (t // QUARTER) + 2, 2 * QUARTERS))
                pool.wait_ge(s["state"], c.count(t + 1, STEPS + 1))
                at = (t % (2 * QUARTER)) * STATE
                tt(plus_kv[:, (t % 2) * STATE:(t % 2 + 1) * STATE], st(t), kv[:, at:at + STATE],
                   ALU.add).then_inc(s["plus_kv"], 1)
                if t == 0 and c.has(1):
                    read_out(c + -1, STEPS // 2 - 1)
                if t and t % 2 == 0:
                    read_out(c, t // 2 - 1)
                for stage in stages:
                    stage.upto(t)

            def pre(c):
                now = settled(pool, c.count())
                yield 17
                pool.wait_ge(s["ka_f"], now)
                pool.wait_ge(s["key"], now)
                tt(k2[:], key[:], k2[:], ALU.mult).then_inc(s["k2"], 1)
                yield 21
                pool.wait_ge(s["p"], now)
                pool.wait_ge(s["rec"], now)
                tt(r_t[c.slot][:], rec[:], p_all[c.slot][:, B:B + COLS], ALU.mult).then_inc(s["r_t"], 1)
                yield 27
                pool.wait_ge(s["consts_in"], 32)
                pool.wait_ge(s["bonus"], now)
                ts(bonus[c.slot][:], bonus[c.slot][:], 1.0, v("gn_b"), ALU.mult, ALU.add).then_inc(s["bonus_b"], 1)
                yield 28

            def mid(c):
                now = settled(pool, c.count())
                last = settled(pool, (c + -1).count()) if c.has(1) else None
                if isinstance(c.base, int) and c.off == CHUNKS - 1:
                    pool.wait_ge(s["state"], CHUNKS * (STEPS + 1))
                    read_out(c, STEPS // 2 - 1)
                yield 11
                pool.wait_ge(s["gaff"], now)
                pool.wait_ge(s["gate"], now)
                tt(z_m[:], z_m[:], gate[c.slot][:], ALU.mult).then_inc(s["gg"], 1)
                yield 19
                pool.wait_ge(s["x2"], now)
                pool.wait_ge(s["x_res"], c.count(16, 16))
                if c.has(1):
                    pool.wait_ge(s["y1"], last)
                tt(x2x[c.slot][:], x2[:], x_res[c.slot][:], ALU.add).then_inc(s["x2x"], 1)
                yield 20

            def fin(c):
                now = settled(pool, c.count())
                last = settled(pool, (c + -1).count()) if c.has(1) else None
                yield 25
                pool.wait_ge(s["consts_in"], 32)
                pool.wait_ge(s["y1"], now)
                if c.has(1):
                    pool.wait_ge(s["res"], last)
                ts(y1b[:], y1[:], 1.0, v("ln_beta"), ALU.mult, ALU.add).then_inc(s["y1b"], 1)
                yield 26

            pipeline(nc.gpsimd, fill, [(1, pre), (-1, mid), (-2, fin)], scan_step, lambda: None)


def constants():
    eye = np.eye(C, dtype=np.float32)
    head = np.kron(np.eye(H, dtype=np.float32), np.ones((N, N), np.float32))
    parts = {"center": eye - 1.0 / C, "mean": np.full((C, C), 1.0 / C),
             "mean8": head / N, "sum8": head, "ident": eye,
             "rank": np.tile(np.arange(E, 0, -1, dtype=np.float32), (128, 4))}
    gather = [np.kron(np.eye(H), np.tile(np.eye(N)[i] - 1.0 / N, (N, 1))) for i in range(N)]
    parts["gather"] = np.concatenate(gather, 1)
    return np.ascontiguousarray(np.concatenate([parts[name] for name in K], 1).astype(np.float32))


def kernel(**inputs):
    import concourse.bacc as bacc
    from concourse.bass_utils import run_bass_kernel_spmd

    a = {name: np.asarray(value) for name, value in inputs.items()}
    attn = lambda name: a["L0_attn_" + name]
    blocks = lambda m: m.reshape(J, C, C).transpose(1, 0, 2).reshape(C, J * C)
    mats = np.concatenate([
        attn("W_k"), attn("w1"), attn("a1"), attn("W_v"), attn("W_r"), attn("g1"), attn("g2"), attn("W_o"),
        np.concatenate([attn("w2"), attn("a2")], 0),
        attn("W_ffn1"), blocks(attn("W_ffn2")), a["L0_ffn_W_router"],
        a["L0_ffn_W1"].transpose(1, 0, 2).reshape(C, E * I), blocks(a["L0_ffn_Wo"])], 1)
    vecs = np.stack([attn(name).reshape(C) for name in VECS] + [a["L0_ffn_" + name] for name in FFN_VECS], 1)
    arrays = {
        "xT": attn("x").transpose(2, 1, 0).reshape(C, T * B),
        "mats": mats,
        "vecs": vecs,
        "consts": constants(),
        "b1": a["L0_ffn_b1"],
    }
    arrays = {name: np.ascontiguousarray(value) for name, value in arrays.items()}
    nc = bacc.Bacc("TRN2", target_bir_lowering=False, num_devices=1)
    aps = [nc.dram_tensor(name, value.shape, F32, kind="ExternalInput").ap() for name, value in arrays.items()]
    out = nc.dram_tensor("outT", (C, T * B), F32, kind="ExternalOutput").ap()
    build(nc, *aps, out)
    result = run_bass_kernel_spmd(nc, [arrays], core_ids=[0])
    return np.asarray(result.results[0]["outT"]).reshape(C, T, B).transpose(2, 1, 0)
```
